# Optimizing a Trainium2 kernel written in Bass

```python
import numpy as np
import jax
import jax.numpy as jnp

def _softmax(x, axis=-1):
    return jax.nn.softmax(x, axis=axis)

def _gelu(x):
    return jax.nn.gelu(x, approximate=True)

def _silu(x):
    return jax.nn.silu(x)

def _sigmoid(x):
    return jax.nn.sigmoid(x)

def _layernorm(x, axis=-1, eps=1e-05):
    m = jnp.mean(x, axis=axis, keepdims=True)
    v = jnp.var(x, axis=axis, keepdims=True)
    return (x - m) / jnp.sqrt(v + eps)

def _scatter_add(tgt, idx, src, axis=0):
    return tgt.at[idx].add(src)

def _segment_sum(src, seg, n):
    return jax.ops.segment_sum(src, seg, n)
kernel_name = 'mk_gps_d1_gnn_r8_b37126'

def setup_inputs(seed: int=0):
    np.random.seed(seed)
    _w = jnp.asarray

    def _rec_inputs():
        import jax
        import jax.numpy as jnp
        _gk = jax.random.key(seed)
        x = -0.0002117 + 1 * jax.random.normal(jax.random.fold_in(_gk, 1), (6250, 256), jnp.float32)
        src = jax.random.randint(jax.random.fold_in(_gk, 2), (100000,), 0, 6250, jnp.int32)
        dst = jnp.minimum((6250 * jax.random.uniform(jax.random.fold_in(_gk, 3), (100000,)) ** 2.0).astype(jnp.int32), 49999)
        _o = jnp.argsort(dst, stable=True)
        src = src[_o]
        dst = dst[_o]
        return (x, src, dst)
    x, src, dst = _rec_inputs()

    def _L0_gnn_setup():
        import jax, jax.numpy as jnp
        import numpy as np
        N = 12500
        E = 200000
        D = 256
        BN_EPS = 1e-05
        key = jax.random.key(seed)
        ks = jax.random.split(key, 6)
        node_feats = jax.random.normal(ks[0], (N, D), dtype=jnp.float32)
        src = jax.random.randint(ks[1], (E,), 0, N, dtype=jnp.int64)
        dst = jax.random.randint(ks[2], (E,), 0, N, dtype=jnp.int64)
        eps = jnp.zeros((1,), dtype=jnp.float32)
        W1 = jax.random.normal(ks[3], (D, 2 * D), dtype=jnp.float32) * (1.0 / np.sqrt(D))
        b1 = jnp.zeros((2 * D,), dtype=jnp.float32)
        W2 = jax.random.normal(ks[4], (2 * D, D), dtype=jnp.float32) * (1.0 / np.sqrt(2 * D))
        b2 = jnp.zeros((D,), dtype=jnp.float32)
        gamma = jnp.ones((D,), dtype=jnp.float32)
        beta = jnp.zeros((D,), dtype=jnp.float32)
        return {'node_feats': node_feats, 'src': src, 'dst': dst, 'eps': eps, 'W1': W1, 'b1': b1, 'W2': W2, 'b2': b2, 'gamma': gamma, 'beta': beta}
    _L0_gnn_all = _L0_gnn_setup()
    _L0_gnn_in = {k: v for k, v in _L0_gnn_all.items() if k in ('eps', 'W1', 'b1', 'W2', 'b2', 'gamma', 'beta')}
    del _L0_gnn_all

    def _L0_mix_setup():
        import jax, jax.numpy as jnp
        import numpy as np
        MIDC = 256
        HEADS = 8
        HEADC = MIDC // HEADS
        EPS = 1e-05

        def _ln(x, gamma, beta):
            mu = jnp.mean(x, axis=-1, keepdims=True)
            var = jnp.var(x, axis=-1, keepdims=True)
            return (x - mu) * jax.lax.rsqrt(var + EPS) * gamma + beta
        key = jax.random.key(seed)
        ks = jax.random.split(key, 8)
        B, HW, C = (8, 512, MIDC)
        s = 1.0 / np.sqrt(C)
        return {'x': jax.random.normal(ks[0], (B, HW, C), jnp.float32), 'w_qkv': jax.random.normal(ks[1], (C, 3 * C), jnp.float32) * s, 'b_qkv': jnp.zeros((3 * C,), jnp.float32), 'kln_g': jnp.ones((HEADC,), jnp.float32), 'kln_b': jnp.zeros((HEADC,), jnp.float32), 'vln_g': jnp.ones((HEADC,), jnp.float32), 'vln_b': jnp.zeros((HEADC,), jnp.float32), 'w1': jax.random.normal(ks[2], (C, C), jnp.float32) * s, 'b1': jnp.zeros((C,), jnp.float32), 'w2': jax.random.normal(ks[3], (C, C), jnp.float32) * s, 'b2': jnp.zeros((C,), jnp.float32)}
    _L0_mix_all = _L0_mix_setup()
    _L0_mix_in = {k: v for k, v in _L0_mix_all.items() if k in ('w_qkv', 'b_qkv', 'kln_g', 'kln_b', 'vln_g', 'vln_b', 'w1', 'b1', 'w2', 'b2')}
    del _L0_mix_all

    def _L0_ffn_setup():
        import jax, jax.numpy as jnp
        import numpy as np
        B, T, D, H, L = (16, 512, 256, 256, 2)

        def _lstm(x, W_ih, W_hh, b_ih, b_hh):
            x_proj = jnp.einsum('btd,gd->btg', x, W_ih) + b_ih + b_hh
            h0 = jnp.zeros((x.shape[0], W_hh.shape[1]), x.dtype)
            c0 = jnp.zeros_like(h0)

            def step(carry, xp):
                h, c = carry
                gates = xp + h @ W_hh.T
                i, f, g, o = jnp.split(gates, 4, axis=-1)
                c = jax.nn.sigmoid(f) * c + jax.nn.sigmoid(i) * jnp.tanh(g)
                h = jax.nn.sigmoid(o) * jnp.tanh(c)
                return ((h, c), h)
            _, hs = jax.lax.scan(step, (h0, c0), jnp.swapaxes(x_proj, 0, 1))
            return jnp.swapaxes(hs, 0, 1)
        key = jax.random.key(seed)
        ks = jax.random.split(key, 9)
        s = 1.0 / np.sqrt(H)
        u = lambda k, shape: jax.random.uniform(k, shape, jnp.float32, -s, s)
        return {'x': jax.random.normal(ks[0], (B, T, D), jnp.float32), 'W_ih': u(ks[1], (4 * H, D)), 'W_hh': u(ks[2], (4 * H, H)), 'b_ih': u(ks[3], (4 * H,)), 'b_hh': u(ks[4], (4 * H,)), 'W_lin': u(ks[5], (L, H)), 'b_lin': u(ks[6], (L,)), 'fw_att': jnp.full((1, H), 0.001, jnp.float32), 'bw_att': jnp.full((1, H), 0.001, jnp.float32)}
    _L0_ffn_all = _L0_ffn_setup()
    _L0_ffn_in = {k: v for k, v in _L0_ffn_all.items() if k in ('W_ih', 'W_hh', 'b_ih', 'b_hh', 'W_lin', 'b_lin', 'fw_att', 'bw_att')}
    del _L0_ffn_all
    return {'x': x, 'src': src, 'dst': dst, 'L0_gnn_eps': _L0_gnn_in['eps'], 'L0_gnn_W1': _L0_gnn_in['W1'], 'L0_gnn_b1': _L0_gnn_in['b1'], 'L0_gnn_W2': _L0_gnn_in['W2'], 'L0_gnn_b2': _L0_gnn_in['b2'], 'L0_gnn_gamma': _L0_gnn_in['gamma'], 'L0_gnn_beta': _L0_gnn_in['beta'], 'L0_mix_w_qkv': _L0_mix_in['w_qkv'], 'L0_mix_b_qkv': _L0_mix_in['b_qkv'], 'L0_mix_kln_g': _L0_mix_in['kln_g'], 'L0_mix_kln_b': _L0_mix_in['kln_b'], 'L0_mix_vln_g': _L0_mix_in['vln_g'], 'L0_mix_vln_b': _L0_mix_in['vln_b'], 'L0_mix_w1': _L0_mix_in['w1'], 'L0_mix_b1': _L0_mix_in['b1'], 'L0_mix_w2': _L0_mix_in['w2'], 'L0_mix_b2': _L0_mix_in['b2'], 'L0_ffn_W_ih': _L0_ffn_in['W_ih'], 'L0_ffn_W_hh': _L0_ffn_in['W_hh'], 'L0_ffn_b_ih': _L0_ffn_in['b_ih'], 'L0_ffn_b_hh': _L0_ffn_in['b_hh'], 'L0_ffn_W_lin': _L0_ffn_in['W_lin'], 'L0_ffn_b_lin': _L0_ffn_in['b_lin'], 'L0_ffn_fw_att': _L0_ffn_in['fw_att'], 'L0_ffn_bw_att': _L0_ffn_in['bw_att']}

def reference(x, src, dst, L0_gnn_eps, L0_gnn_W1, L0_gnn_b1, L0_gnn_W2, L0_gnn_b2, L0_gnn_gamma, L0_gnn_beta, L0_mix_w_qkv, L0_mix_b_qkv, L0_mix_kln_g, L0_mix_kln_b, L0_mix_vln_g, L0_mix_vln_b, L0_mix_w1, L0_mix_b1, L0_mix_w2, L0_mix_b2, L0_ffn_W_ih, L0_ffn_W_hh, L0_ffn_b_ih, L0_ffn_b_hh, L0_ffn_W_lin, L0_ffn_b_lin, L0_ffn_fw_att, L0_ffn_bw_att):
    import jax
    import jax.numpy as jnp

    def _L0_gnn_ref(node_feats, src, dst, eps, W1, b1, W2, b2, gamma, beta):
        import jax, jax.numpy as jnp
        import numpy as np
        N = 12500
        E = 200000
        D = 256
        BN_EPS = 1e-05
        n = node_feats.shape[0]
        neigh = jax.ops.segment_sum(node_feats[src], dst, num_segments=n)
        h = (1.0 + eps) * node_feats + neigh
        h = jax.nn.relu(h @ W1 + b1) @ W2 + b2
        mean = jnp.mean(h, axis=0)
        var = jnp.mean(jnp.square(h - mean), axis=0)
        h = (h - mean) * jax.lax.rsqrt(var + BN_EPS) * gamma + beta
        return h

    def _L0_mix_ref(x, w_qkv, b_qkv, kln_g, kln_b, vln_g, vln_b, w1, b1, w2, b2):
        import jax, jax.numpy as jnp
        import numpy as np
        MIDC = 256
        HEADS = 8
        HEADC = MIDC // HEADS
        EPS = 1e-05

        def _ln(x, gamma, beta):
            mu = jnp.mean(x, axis=-1, keepdims=True)
            var = jnp.var(x, axis=-1, keepdims=True)
            return (x - mu) * jax.lax.rsqrt(var + EPS) * gamma + beta
        B, HW, C = x.shape
        bias = x
        qkv = (x @ w_qkv + b_qkv).reshape(B, HW, HEADS, 3 * HEADC)
        qkv = qkv.transpose(0, 2, 1, 3)
        q, k, v = jnp.split(qkv, 3, axis=-1)
        k = _ln(k, kln_g, kln_b)
        v = _ln(v, vln_g, vln_b)
        kv = jnp.einsum('bhnd,bhne->bhde', k, v) / HW
        out = jnp.einsum('bhnd,bhde->bhne', q, kv)
        out = out.transpose(0, 2, 1, 3).reshape(B, HW, C)
        ret = out + bias
        h = jax.nn.gelu(ret @ w1 + b1, approximate=False)
        return h @ w2 + b2 + bias

    def _L0_ffn_ref(x, W_ih, W_hh, b_ih, b_hh, W_lin, b_lin, fw_att, bw_att):
        import jax, jax.numpy as jnp
        import numpy as np
        B, T, D, H, L = (16, 512, 256, 256, 2)

        def _lstm(x, W_ih, W_hh, b_ih, b_hh):
            x_proj = jnp.einsum('btd,gd->btg', x, W_ih) + b_ih + b_hh
            h0 = jnp.zeros((x.shape[0], W_hh.shape[1]), x.dtype)
            c0 = jnp.zeros_like(h0)

            def step(carry, xp):
                h, c = carry
                gates = xp + h @ W_hh.T
                i, f, g, o = jnp.split(gates, 4, axis=-1)
                c = jax.nn.sigmoid(f) * c + jax.nn.sigmoid(i) * jnp.tanh(g)
                h = jax.nn.sigmoid(o) * jnp.tanh(c)
                return ((h, c), h)
            _, hs = jax.lax.scan(step, (h0, c0), jnp.swapaxes(x_proj, 0, 1))
            return jnp.swapaxes(hs, 0, 1)
        lstm_out = _lstm(x, W_ih, W_hh, b_ih, b_hh)
        logits = jnp.einsum('bth,lh->btl', lstm_out, W_lin) + b_lin
        g = jax.lax.stop_gradient(jnp.argmax(logits, axis=-1).astype(lstm_out.dtype))[..., None]
        w = g * lstm_out
        inc = jnp.cumsum(w, axis=1)
        prefix = inc - w
        suffix = inc[:, -1:, :] - inc
        return 2.0 * lstm_out + prefix * fw_att + suffix * bw_att
    xn = _layernorm(x, axis=-1)
    x = x + _L0_gnn_ref(xn, src, dst, L0_gnn_eps, L0_gnn_W1, L0_gnn_b1, L0_gnn_W2, L0_gnn_b2, L0_gnn_gamma, L0_gnn_beta) + _L0_mix_ref(xn[None], L0_mix_w_qkv, L0_mix_b_qkv, L0_mix_kln_g, L0_mix_kln_b, L0_mix_vln_g, L0_mix_vln_b, L0_mix_w1, L0_mix_b1, L0_mix_w2, L0_mix_b2)[0]
    x = x + _L0_ffn_ref(_layernorm(x, axis=-1)[None], L0_ffn_W_ih, L0_ffn_W_hh, L0_ffn_b_ih, L0_ffn_b_hh, L0_ffn_W_lin, L0_ffn_b_lin, L0_ffn_fw_att, L0_ffn_bw_att)[0]
    return x

_drawn_inputs = setup_inputs


def setup_inputs(seed=0):
    import zlib

    import numpy as np

    out = dict(_drawn_inputs(seed))
    spreads = {'L0_gnn_b1': (0.0, 0.8),
     'L0_gnn_b2': (0.0, 0.8),
     'L0_gnn_gamma': (1.0, 0.2),
     'L0_gnn_beta': (0.0, 0.1),
     'L0_mix_b_qkv': (0.0, 0.288),
     'L0_mix_kln_g': (1.0, 0.6),
     'L0_mix_kln_b': (0.0, 0.489),
     'L0_mix_vln_g': (1.0, 0.6),
     'L0_mix_vln_b': (0.0, 0.439),
     'L0_mix_b1': (0.0, 0.278),
     'L0_mix_b2': (0.0, 0.1),
     'L0_ffn_fw_att': (0.0010000000474974513, 0.6),
     'L0_ffn_bw_att': (0.0010000000474974513, 0.6)}
    factors = {'L0_ffn_b_ih': 3.24, 'L0_ffn_b_hh': 2.996, 'L0_ffn_W_lin': 5.718}
    for name, (base, spread) in spreads.items():
        noise = np.random.default_rng([zlib.crc32(name.encode()), seed]).standard_normal(out[name].shape)
        drawn = base * np.exp(spread * noise) if base else spread * noise
        out[name] = jnp.asarray(drawn.astype(out[name].dtype))
    for name, factor in factors.items():
        out[name] = (out[name] * factor).astype(out[name].dtype)
    return out
```

```python
from contextlib import ExitStack

import concourse.bass as bass
from concourse import mybir

F32 = mybir.dt.float32
BF16 = mybir.dt.bfloat16
I32 = mybir.dt.int32
ALU = mybir.AluOpType
ACT = mybir.ActivationFunctionType
AX = mybir.AxisListType

N, D, E = 6250, 256, 100000
KD = D // 128
R = 125
NT = N // R
C = 250
NC = N // C
XL = 5
HEADS, HC = 8, D // 8
FF = 2 * D
MF = FF // 128
GT = 4
NG = E // (R * GT)
NA = 2
G4 = 4 * D
GC = G4 // 128
IFG = 6
B = 5
NB = N // B
NI = NB // 2
PARTS = 3
LN_EPS = 1e-5
MIX_LOADS = 24


REFINE_STEPS = 5


def due(count):
    return not isinstance(count, int) or count > 0


def first_apart(engine, steps, body):
    body(0)
    with engine.Fori(1, steps, 1) as i:
        body(i)


def refine_rsqrt(nc, step, y, root, v, t):
    step(nc.vector.reciprocal(y, root))
    step(nc.vector.tensor_tensor(t, y, y, ALU.mult))
    step(nc.vector.tensor_tensor(t, t, v, ALU.mult))
    step(nc.vector.tensor_scalar(t, t, -0.5, 1.5, ALU.mult, ALU.add))
    step(nc.vector.tensor_tensor(y, y, t, ALU.mult))


def gps_layer_kernel(nc, x, src, dst, gnn_eps, gW1, gb1, gW2, gb2, gamma, beta, w_qkv, b_qkv,
                     kln_g, kln_b, vln_g, vln_b, mw1, mb1, mw2, mb2, W_ih, W_hh, b_ih, b_hh,
                     W_lin, b_lin, fw_att, bw_att, out):
    xn_d = nc.dram_tensor("xn_d", (N, D), F32, kind="Internal").ap()
    acc_d = [nc.dram_tensor(f"acc{a}_d", (N + R, D), F32, kind="Internal").ap() for a in range(NA)]
    x2_d = nc.dram_tensor("x2_d", (128, (NB + 2) * KD * B * PARTS), BF16, kind="Internal").ap()

    top = ExitStack()
    stage = ExitStack()

    def open_block():
        stage.close()
        return stage.enter_context(nc.Block())

    with top, stage, nc.allow_non_contiguous_dma(reason="vectors of 256 numbers, loaded once"):
        def sem(name):
            return top.enter_context(nc.semaphore(name))

        def sb(name, shape, dt=F32, ctx=top):
            return ctx.enter_context(nc.sbuf_tensor(name, shape, dt))

        sp_turn, pool_turn = sem("sp_turn"), sem("pool_turn")

        bank = [top.enter_context(nc.psum_tensor(f"bank{i}", [128, 512], F32)) for i in range(8)]

        XT = sb("XT", [128, KD, N])
        U = sb("U", [128, KD, N])
        Hs = U[:, :, :].rearrange("p k n -> p (k n)").rearrange("p (t k) -> p t k", k=KD)
        whh = sb("whh", [128, PARTS, KD, G4], BF16)
        wih = sb("wih", [128, PARTS, KD, G4], BF16)
        gbias = sb("gbias", [128, G4], BF16)
        ident = sb("ident", [128, 128])
        kvsum = sb("kvsum", [128, KD, 128])

        stage.close()

        with ExitStack() as st:
            scratch = U[:, :, :].rearrange("p k n -> p (k n)")
            wraw = [scratch[:, w * GC * D:(w + 1) * GC * D].rearrange("p (c d) -> p c d", c=GC) for w in range(2)]
            wT = scratch[:, 4096:5120].rearrange("p (u n) -> p u n", u=2)
            wres = scratch[:, 5120:5632]
            brow = scratch[0:1, 5632:5632 + 2 * G4].rearrange("p (a n) -> p a n", a=2)
            bres = scratch[0:1, 7680:7680 + G4]
            ZW = (N + R) * D // R // 8
            zero = sb("zero", [R, ZW], F32, st)
            zero16 = sb("zero16", [128, 2 * KD * B * PARTS], BF16, st)
            one_eps = sb("one_eps", [R, 1], F32, st)
            xall = sb("xall", [R, NT, D], F32, st)
            xn = sb("xn", [R, 2, D], F32, st)
            a0 = sb("a0", [R, 2, D], F32, st)
            xs = sb("xs", [R, 2, D], F32, st)
            stats = sb("stats", [R, NT, 6], F32, st)
            mv = sb("mv", [R, NT, 2], F32, st)
            var = sb("var", [R, NT], F32, st)
            root = sb("root", [R, NT], F32, st)
            rstd = sb("rstd", [R, NT], F32, st)
            ntmp = sb("ntmp", [R, NT], F32, st)
            w_in, b_in, eps_in = sem("w_in"), sem("b_in"), sem("eps_in")
            x_in = [sem(f"x_in{j}") for j in range(XL)]
            var_ready, root_ready = sem("var_ready"), sem("root_ready")
            zeroed, ident0, ident_ready = sem("zeroed"), sem("ident0"), sem("ident_ready")
            zero_out = sem("zero_out")
            xn_out = [sem(f"xn_out{b}") for b in range(2)]
            w_turned, w_scaled, w_split = sem("w_turned"), sem("w_scaled"), sem("w_split")
            set_chain = sem("set_chain")
            xn_ready, xs_ready = sem("xn_ready"), sem("xs_ready")
            a0_ready = sem("a0_ready")
            x_turned, x_copied = sem("x_turned"), sem("x_copied")
            stats_made, mv_made = sem("stats_made"), sem("mv_made")

            SET_LINKS = 10 + 3 * 8 + REFINE_STEPS

            block = open_block()

            @block.sync
            def _(sp):
                xt = x.rearrange("(t p) d -> p t d", p=R)
                for j in range(XL):
                    at = slice(j * NT // XL, (j + 1) * NT // XL)
                    sp.dma_start(xall[:, at, :], xt[:, at, :]).then_inc(x_in[j], 16)
                for w, src_w in enumerate((W_hh, W_ih)):
                    sp.dma_start(wraw[w], src_w.rearrange("(c p) d -> p c d", p=128)).then_inc(w_in, 16)
                sp.dma_start(brow[:, 0, :], b_ih.rearrange("(a n) -> a n", a=1)).then_inc(b_in, 16)
                sp.dma_start(brow[:, 1, :], b_hh.rearrange("(a n) -> a n", a=1)).then_inc(b_in, 16)
                sp.dma_start(one_eps[:], gnn_eps.rearrange("(a n) -> a n", a=1).broadcast_to([R, 1])).then_inc(eps_in, 16)
                sp.wait_ge(zeroed, 2)
                flat = acc_d[1].rearrange("(p r) d -> p (r d)", p=R)
                for j in range(8):
                    sp.dma_start(flat[:, j * ZW:(j + 1) * ZW], zero[:]).then_inc(zero_out, 16)
                sp.dma_start(acc_d[0][N:N + R, :], zero[:, 0:D]).then_inc(zero_out, 16)
                sp.dma_start(x2_d[:, NB * KD * B * PARTS:], zero16[:]).then_inc(zero_out, 16)
                def body(i):
                    for b in range(2):
                        sp.wait_ge(a0_ready, 2 * i + b + 1)
                        sp.sem_inc(sp_turn)
                        sp.dma_start(xn_d[bass.ds((2 * i + b) * R, R), :], xn[:, b, :]).then_inc(xn_out[b], 16)
                        sp.dma_start(acc_d[0][bass.ds((2 * i + b) * R, R), :], a0[:, b, :]).then_inc(xn_out[b], 16)

                first_apart(sp, NT // 2, body)
                for b in range(2):
                    sp.wait_ge(xn_out[b], 32 * (NT // 2))
                sp.wait_ge(zero_out, 16 * 10)

            @block.gpsimd
            def _(pool):
                nc.gpsimd.memset(ident[:], 0.0).then_inc(ident0, 1)
                pool.wait_ge(ident0, 1)
                nc.gpsimd.affine_select(out=ident[:], in_=ident[:], compare_op=ALU.not_equal, fill=1.0, base=0,
                                        pattern=[[-1, 128]], channel_multiplier=1).then_inc(ident_ready, 1)

            @block.tensor
            def _(pe):
                pe.wait_ge(w_in, 32)
                pe.wait_ge(ident_ready, 1)
                for u in range(8):
                    w, k, half = u // 4, u // 2 % 2, u % 2
                    if u >= 2:
                        pe.wait_ge(w_scaled, u - 1)
                    for j in range(4):
                        last = nc.tensor.transpose(bank[u % 2][:, j * 128:(j + 1) * 128],
                                                   wraw[w][:, 4 * half + j, k * 128:(k + 1) * 128], ident[:])
                    last.then_inc(w_turned, 1)
                def body(i):
                    for b in range(2):
                        pe.wait_ge(xs_ready, 2 * i + b + 1)
                        if due(2 * (2 * i + b)):
                            pe.wait_ge(x_copied, 2 * (2 * i + b))
                        for k in range(KD):
                            nc.tensor.transpose(bank[2][:, k * R:(k + 1) * R], xn[:, b, k * 128:(k + 1) * 128],
                                                ident[0:R, 0:R])
                        for k in range(KD):
                            last = nc.tensor.transpose(bank[3][:, k * R:(k + 1) * R],
                                                       xs[:, b, k * 128:(k + 1) * 128], ident[0:R, 0:R])
                        last.then_inc(x_turned, 1)

                first_apart(pe, NT // 2, body)

            @block.scalar
            def _(act):
                for u in range(8):
                    w, half = u // 4, u % 2
                    s = 0.5 if w == 0 else 1.0
                    act.wait_ge(w_turned, u + 1)
                    if u >= 2:
                        act.wait_ge(w_split, u - 1)
                    for lo, hi, f in ((0, 256, 0.5 if half == 0 else 1.0), (256, 512, 0.5)):
                        last = nc.scalar.activation(wT[:, u % 2, lo:hi], bank[u % 2][:, lo:hi], ACT.Copy, scale=f * s)
                    last.then_inc(w_scaled, 1)
                act.wait_ge(var_ready, 1)
                nc.scalar.activation(root[:], var[:], ACT.Sqrt).then_inc(root_ready, 1)
                act.wait_ge(w_split, 8)
                act.wait_ge(set_chain, SET_LINKS)
                def body(i):
                    for b in range(2):
                        act.wait_ge(x_turned, 2 * i + b + 1)
                        at = bass.ds((2 * i + b) * R, R)
                        nc.scalar.activation(U[:, :, at], bank[2][:, 0:KD * R].rearrange("p (k n) -> p k n", k=KD),
                                             ACT.Copy).then_inc(x_copied, 1)
                        nc.scalar.activation(XT[:, :, at], bank[3][:, 0:KD * R].rearrange("p (k n) -> p k n", k=KD),
                                             ACT.Copy).then_inc(x_copied, 1)

                first_apart(act, NT // 2, body)

            @block.vector
            def _(dve):
                nc.vector.memset(zero[:], 0.0).then_inc(zeroed, 1)
                nc.vector.memset(zero16[:], 0.0).then_inc(zeroed, 1)
                count = [0]

                def link(ins):
                    count[0] += 1
                    ins.then_inc(set_chain, 1)
                    dve.wait_ge(set_chain, count[0])

                link(nc.vector.memset(gbias[:], 0.0))
                dve.wait_ge(b_in, 32)
                link(nc.vector.tensor_tensor(brow[:, 0, :], brow[:, 0, :], brow[:, 1, :], ALU.add))
                link(nc.vector.tensor_scalar(brow[:, 0, 0:2 * D], brow[:, 0, 0:2 * D], 0.5, None, ALU.mult))
                link(nc.vector.tensor_scalar(brow[:, 0, 3 * D:], brow[:, 0, 3 * D:], 0.5, None, ALU.mult))
                link(nc.vector.tensor_copy(gbias[0:1, :], brow[:, 0, :]))
                link(nc.vector.tensor_tensor(bres, brow[:, 0, :], gbias[0:1, :], ALU.subtract))
                link(nc.vector.tensor_copy(gbias[32:33, :], bres))
                link(nc.vector.tensor_copy(brow[:, 1, :], gbias[32:33, :]))
                link(nc.vector.tensor_tensor(gbias[64:65, :], bres, brow[:, 1, :], ALU.subtract))
                dve.wait_ge(eps_in, 16)
                link(nc.vector.tensor_scalar(one_eps[:], one_eps[:], 1.0, None, ALU.add))
                for u in range(8):
                    w, k, half = u // 4, u // 2 % 2, u % 2
                    parts = [(whh, wih)[w][:, p, k, half * 512:(half + 1) * 512] for p in range(PARTS)]
                    dve.wait_ge(w_scaled, u + 1)
                    link(nc.vector.tensor_copy(parts[0], wT[:, u % 2, :]))
                    link(nc.vector.tensor_tensor(wres, wT[:, u % 2, :], parts[0], ALU.subtract))
                    link(nc.vector.tensor_copy(parts[1], wres))
                    nc.vector.tensor_tensor(parts[2], wres, parts[1], ALU.subtract).then_inc(w_split, 1)
                dve.wait_ge(w_split, 8)
                for j in range(XL):
                    dve.wait_ge(x_in[j], 16)
                with dve.Fori(0, NT, 1) as t:
                    nc.vector.bn_stats(stats[:, bass.ds(t, 1), :].rearrange("p t s -> p (t s)"),
                                       xall[:, bass.ds(t, 1), :].rearrange("p t d -> p (t d)")).then_inc(stats_made, 1)
                dve.wait_ge(stats_made, NT)
                for t in range(NT):
                    nc.vector.bn_aggr(mv[:, t, :], stats[:, t, :]).then_inc(mv_made, 1)
                dve.wait_ge(mv_made, NT)
                nc.vector.tensor_scalar(var[:], mv[:, :, 1], LN_EPS, None, ALU.add).then_inc(var_ready, 1)
                dve.wait_ge(var_ready, 1)
                dve.wait_ge(root_ready, 1)
                refine_rsqrt(nc, link, rstd[:], root[:], var[:], ntmp[:])
                assert count[0] == SET_LINKS
                def body(i):
                    for b in range(2):
                        t = 2 * i + b
                        tile = xall[:, bass.ds(t, 1), :].rearrange("p t d -> p (t d)")
                        if due(32 * i):
                            dve.wait_ge(xn_out[b], 32 * i)
                        if b == 0:
                            if due(2 * i):
                                dve.wait_ge(x_turned, 2 * i)
                        mean = mv[:, bass.ds(t, 1), 0:1].rearrange("p t o -> p (t o)")
                        nc.vector.tensor_scalar(xn[:, b, :], tile, mean, rstd[:, bass.ds(t, 1)], ALU.subtract,
                                                ALU.mult).then_inc(xn_ready, 1)
                        dve.wait_ge(xn_ready, t + 1)
                        nc.vector.tensor_tensor(xs[:, b, :], tile, xn[:, b, :], ALU.add).then_inc(xs_ready, 1)
                        nc.vector.tensor_scalar(a0[:, b, :], xn[:, b, :], one_eps[:], None,
                                                ALU.mult).then_inc(a0_ready, 1)

                first_apart(dve, NT // 2, body)

        stage.close()

        with ExitStack() as st:
            staged_i = sb("staged_i", [R, 2, 2, GT], I32, st)
            dstf = sb("dstf", [R, 2, GT], F32, st)
            equal = sb("equal", [R, 2, GT, R], F32, st)
            earlier = sb("earlier", [R, GT, R], F32, st)
            below = sb("below", [R, R], F32, st)
            spare_i = sb("spare_i", [R, 1], I32, st)
            spare = sb("spare", [R, 1], F32, st)
            dup = sb("dup", [R, GT], F32, st)
            move = sb("move", [R, GT], F32, st)
            target = sb("target", [R, 2, GT], I32, st)
            rows = sb("rows", [R, 2, GT, D], F32, st)
            sums = sb("sums", [R, 2, GT, D], F32, st)

            wq = sb("wq", [128, KD, HEADS, HC], F32, st)
            wkv = sb("wkv", [128, KD, 2, HEADS, HC], F32, st)
            bq = sb("bq", [128, KD], F32, st)
            bkv = sb("bkv", [R, 2, HEADS, HC], F32, st)
            kv_g = sb("kv_g", [R, 2, HEADS, HC], F32, st)
            kv_b = sb("kv_b", [R, 2, HEADS, HC], F32, st)
            w1 = sb("w1", [128, KD, D], F32, st)
            w2 = sb("w2", [128, KD, D], F32, st)
            b1 = sb("b1", [128, KD], F32, st)
            b2 = sb("b2", [128, KD], F32, st)
            xk = sb("xk", [128, KD, R], F32, st)
            kv = sb("kv", [R, 2 * HEADS, HC], F32, st)
            cen = sb("cen", [R, 2 * HEADS, HC], F32, st)
            sq = sb("sq", [R, 2 * HEADS, HC], F32, st)
            gsum = sb("gsum", [R, 2 * HEADS], F32, st)
            gvar, groot, grstd, gtmp = (sb(n, [R, 2 * HEADS], F32, st) for n in ("gvar", "groot", "grstd", "gtmp"))
            kvn = sb("kvn", [R, 2 * HEADS, HC], F32, st)
            attn = sb("attn", [128, KD, 128], F32, st)
            qs = sb("qs", [128, KD, C], F32, st)
            rt = sb("rt", [128, KD, C], F32, st)
            hm = sb("hm", [128, KD, C], F32, st)

            staged = [sem(f"staged{g}") for g in range(2)]
            gathered = [sem(f"gathered{g}") for g in range(2)]
            scattered = [[sem(f"scattered{a}_{g}") for g in range(2)] for a in range(NA)]
            cast, dst_turned = sem("cast"), sem("dst_turned")
            equal_ready, target_ready = sem("equal_ready"), sem("target_ready")
            summed, sums_copied = sem("summed"), sem("sums_copied")
            edge_chain = sem("edge_chain")
            below0, below1, spare0, spare1 = sem("below0"), sem("below1"), sem("spare0"), sem("spare1")
            mixw_in, kv_chain = sem("mixw_in"), sem("kv_chain")
            xk_in, kv_made, kv_read = sem("xk_in"), sem("kv_made"), sem("kv_read")
            cen_ready, sq_ready, kvn_ready = sem("cen_ready"), sem("sq_ready"), sem("kvn_ready")
            gvar_ready, groot_ready = sem("gvar_ready"), sem("groot_ready")
            kv_prod, kv_added, kvsum0 = sem("kv_prod"), sem("kv_added"), sem("kvsum0")
            attn0, attn_ready = sem("attn0"), sem("attn_ready")
            q_made, q_ready, r_made, r_ready = sem("q_made"), sem("q_ready"), sem("r_made"), sem("r_ready")
            h_made, h_ready, m_made, m_added = sem("h_made"), sem("h_ready"), sem("m_made"), sem("m_added")

            turned = bank[0][0:R, 0:GT * R].rearrange("p (t n) -> p t n", t=GT)
            prod = [bank[1 + m][0:R, :].rearrange("p (t d) -> p t d", t=2) for m in range(2)]
            src_g = src.rearrange("(q p t) -> q p t", p=R, t=GT)
            dst_g = dst.rearrange("(q p t) -> q p t", p=R, t=GT)

            def stage_group(sp, h, g):
                if due(16 * GT * h):
                    sp.wait_ge(gathered[g], 16 * GT * h)
                sp.sem_inc(sp_turn)
                if due(2 * h):
                    sp.wait_ge(cast, 2 * h)
                sp.sem_inc(sp_turn)
                for s, v in enumerate((src_g, dst_g)):
                    sp.dma_start(staged_i[:, g, s, :], v[bass.ds(2 * h + g, 1)].rearrange("q p t -> p (q t)"))\
                      .then_inc(staged[g], 16)

            def gather_group(pool, h, g, first=False):
                pool.wait_ge(staged[g], 32 * (h + 1))
                if not first and due(2 * h + g - 1):
                    pool.wait_ge(summed, 2 * h + g - 1)
                    pool.sem_inc(pool_turn)
                for j in range(GT):
                    pool.indirect_dma_start(
                        out=rows[:, g, j, :], out_offset=None, in_=xn_d,
                        in_offset=bass.IndirectOffsetOnAxis(ap=staged_i[:, g, 0, j:j + 1], axis=0),
                    ).then_inc(gathered[g], 16)

            def scatter_group(pool, h, g):
                pool.wait_ge(target_ready, 2 * h + g + 1)
                pool.wait_ge(sums_copied, 2 * (2 * h + g + 1))
                pool.sem_inc(pool_turn)
                for j in range(GT):
                    a = j % NA
                    if j >= NA:
                        pool.wait_ge(scattered[a][g], 32 * h + 16)
                        pool.sem_inc(pool_turn)
                    elif g:
                        pool.wait_ge(scattered[a][0], 32 * (h + 1))
                        pool.sem_inc(pool_turn)
                    else:
                        if due(32 * h):
                            pool.wait_ge(scattered[a][1], 32 * h)
                        pool.sem_inc(pool_turn)
                    pool.indirect_dma_start(
                        out=acc_d[a], out_offset=bass.IndirectOffsetOnAxis(ap=target[:, g, j:j + 1], axis=0),
                        in_=sums[:, g, j, :], in_offset=None, compute_op=ALU.add,
                    ).then_inc(scattered[a][g], 16)

            def turn_targets(pe, h, g):
                pe.wait_ge(cast, 2 * h + g + 1)
                if due(2 * h + g):
                    pe.wait_ge(equal_ready, 2 * h + g)
                for j in range(GT):
                    last = nc.tensor.transpose(turned[:, j, :], dstf[:, g, j:j + 1].broadcast_to([R, R]),
                                               ident[0:R, 0:R])
                last.then_inc(dst_turned, 1)

            def sum_equal(pe, h, g):
                pe.wait_ge(equal_ready, 2 * h + g + 1)
                pe.wait_ge(gathered[g], 16 * GT * (h + 1))
                if due(2 * (2 * h + g)):
                    pe.wait_ge(sums_copied, 2 * (2 * h + g))
                for j in range(GT):
                    last = nc.tensor.matmul(prod[j // 2][:, j % 2, :], equal[:, g, j, :], rows[:, g, j, :],
                                            start=True, stop=True)
                last.then_inc(summed, 1)

            def copy_sums(act, h, g):
                act.wait_ge(summed, 2 * h + g + 1)
                for a in range(NA):
                    if due(32 * h):
                        act.wait_ge(scattered[a][g], 32 * h)
                for m in range(2):
                    nc.scalar.activation(sums[:, g, 2 * m:2 * m + 2, :], prod[m], ACT.Copy).then_inc(sums_copied, 1)

            EDGE_LINKS = 3

            def cast_targets(dve, h, g):
                dve.wait_ge(staged[g], 32 * (h + 1))
                if due(2 * h):
                    dve.wait_ge(target_ready, 2 * h)
                nc.vector.tensor_copy(dstf[:, g, :], staged_i[:, g, 1, :]).then_inc(cast, 1)

            def find_equal(dve, h, g):
                q = 2 * h + g
                done = [0]

                def step(ins):
                    done[0] += 1
                    ins.then_inc(edge_chain, 1)
                    dve.wait_ge(edge_chain, EDGE_LINKS * q + done[0])

                mine = dstf[:, g, :].rearrange("p (t o) -> p t o", o=1).broadcast_to([R, GT, R])
                dve.wait_ge(dst_turned, q + 1)
                if due(2 * h):
                    dve.wait_ge(summed, 2 * h)
                nc.vector.tensor_tensor(equal[:, g, :, :], turned, mine, ALU.is_equal).then_inc(equal_ready, 1)
                dve.wait_ge(equal_ready, q + 1)
                step(nc.vector.tensor_tensor(earlier[:], equal[:, g, :, :],
                                             below[:].rearrange("p (o n) -> p o n", o=1).broadcast_to([R, GT, R]),
                                             ALU.mult))
                step(nc.vector.tensor_reduce(dup[:], earlier[:], axis=AX.X, op=ALU.max))
                step(nc.vector.scalar_tensor_tensor(out=move[:], in0=dstf[:, g, :], scalar=spare[:], in1=dup[:],
                                                    op0=ALU.subtract, op1=ALU.mult))
                for a in range(NA):
                    if due(32 * h):
                        dve.wait_ge(scattered[a][g], 32 * h)
                nc.vector.tensor_tensor(target[:, g, :], dstf[:, g, :], move[:], ALU.subtract).then_inc(target_ready, 1)
                assert done[0] == EDGE_LINKS

            block = open_block()

            H2 = NT

            @block.sync
            def _(sp):
                ld = []
                wv = w_qkv.rearrange("(k p) (h s c) -> p k h s c", p=128, s=3, c=HC)
                for k in range(KD):
                    ld.append((wq[:, k], wv[:, k, :, 0, :]))
                    for s in range(2):
                        ld.append((wkv[:, k, s], wv[:, k, :, s + 1, :]))
                bv = b_qkv.rearrange("(h s c) -> s h c", s=3, c=HC)
                for k in range(KD):
                    for h in range(4):
                        ld.append((bq[32 * h:32 * h + 32, k:k + 1],
                                   bv[0, 4 * k + h, :].rearrange("(c o) -> c o", o=1)))
                for s in range(2):
                    ld.append((bkv[:, s], bv[s + 1:s + 2, :, :].broadcast_to([R, HEADS, HC])))
                for s, (g_, b_) in enumerate(((kln_g, kln_b), (vln_g, vln_b))):
                    for to, v in ((kv_g, g_), (kv_b, b_)):
                        ld.append((to[:, s], v.rearrange("(a o c) -> a o c", a=1, o=1).broadcast_to([R, HEADS, HC])))
                for to, v in ((w1, mw1), (w2, mw2)):
                    ld.append((to[:], v.rearrange("(k p) n -> p k n", p=128)))
                for to, v in ((b1, mb1), (b2, mb2)):
                    ld.append((to[:], v.rearrange("(k p) -> p k", p=128)))
                assert len(ld) == MIX_LOADS
                for to, v in ld:
                    sp.dma_start(to, v).then_inc(mixw_in, 16)
                def body(i):
                    stage_group(sp, i, 0)
                    stage_group(sp, i, 1)
                    if due(i):
                        sp.wait_ge(kv_made, i)
                    sp.sem_inc(sp_turn)
                    sp.dma_start(xk[:], U[:, :, bass.ds(i * R, R)]).then_inc(xk_in, 16)

                first_apart(sp, H2, body)

            @block.gpsimd
            def _(pool):
                nc.gpsimd.memset(below[:], 1.0).then_inc(below0, 1)
                nc.gpsimd.iota(spare_i[:], pattern=[[0, 1]], base=N, channel_multiplier=1).then_inc(spare0, 1)
                pool.wait_ge(below0, 1)
                nc.gpsimd.affine_select(out=below[:], in_=below[:], compare_op=ALU.is_ge, fill=0.0, base=-1,
                                        pattern=[[-1, R]], channel_multiplier=1).then_inc(below1, 1)
                gather_group(pool, 0, 0, first=True)
                def body(i):
                    gather_group(pool, i, 1)
                    scatter_group(pool, i, 0)
                    gather_group(pool, i + 1, 0)
                    scatter_group(pool, i, 1)

                first_apart(pool, H2 - 1, body)
                gather_group(pool, H2 - 1, 1)
                scatter_group(pool, H2 - 1, 0)
                scatter_group(pool, H2 - 1, 1)

            @block.tensor
            def _(pe):
                pe.wait_ge(mixw_in, 16 * MIX_LOADS)
                def body(i):
                    turn_targets(pe, i, 0)
                    pe.wait_ge(xk_in, 16 * (i + 1))
                    if due(i):
                        pe.wait_ge(kv_read, i)
                    for k in range(KD):
                        last = nc.tensor.matmul(bank[3][0:R, :], xk[:, k, :],
                                                wkv[:, k].rearrange("p s h c -> p (s h c)"),
                                                start=k == 0, stop=k == KD - 1)
                    last.then_inc(kv_made, 1)
                    turn_targets(pe, i, 1)
                    sum_equal(pe, i, 0)
                    pe.wait_ge(kvn_ready, i + 1)
                    if due(i):
                        pe.wait_ge(kv_added, i)
                    flat = kvn[:].rearrange("p s c -> p (s c)")
                    for c in range(KD):
                        last = nc.tensor.matmul(bank[4][:, c * 128:(c + 1) * 128], flat[:, c * 128:(c + 1) * 128],
                                                flat[:, D + c * 128:D + (c + 1) * 128], start=True, stop=True)
                    last.then_inc(kv_prod, 1)
                    sum_equal(pe, i, 1)

                first_apart(pe, H2, body)

            @block.scalar
            def _(act):
                def body(i):
                    act.wait_ge(cen_ready, i + 1)
                    nc.scalar.activation(sq[:], cen[:], ACT.Square).then_inc(sq_ready, 1)
                    copy_sums(act, i, 0)
                    act.wait_ge(gvar_ready, i + 1)
                    nc.scalar.activation(groot[:], gvar[:], ACT.Sqrt).then_inc(groot_ready, 1)
                    copy_sums(act, i, 1)

                first_apart(act, H2, body)

            @block.vector
            def _(dve):
                nc.vector.memset(kvsum[:], 0.0).then_inc(kvsum0, 1)
                dve.wait_ge(kvsum0, 1)
                dve.wait_ge(spare0, 1)
                dve.wait_ge(below1, 1)
                nc.vector.tensor_copy(spare[:], spare_i[:]).then_inc(spare1, 1)
                dve.wait_ge(spare1, 1)
                dve.wait_ge(mixw_in, 16 * MIX_LOADS)
                links = 5 + REFINE_STEPS
                def body(i):
                    done = [0]

                    def step(ins):
                        done[0] += 1
                        ins.then_inc(kv_chain, 1)
                        dve.wait_ge(kv_chain, links * i + done[0])

                    def spread(v):
                        return v.rearrange("p (s o) -> p s o", o=1).broadcast_to([R, 2 * HEADS, HC])

                    cast_targets(dve, i, 0)
                    cast_targets(dve, i, 1)
                    find_equal(dve, i, 0)
                    dve.wait_ge(kv_made, i + 1)
                    nc.vector.tensor_tensor(kv[:], bank[3][0:R, :].rearrange("p (s c) -> p s c", c=HC),
                                            bkv[:].rearrange("p s h c -> p (s h) c"), ALU.add).then_inc(kv_read, 1)
                    dve.wait_ge(kv_read, i + 1)
                    step(nc.vector.tensor_reduce(gsum[:], kv[:], axis=AX.X, op=ALU.add))
                    step(nc.vector.tensor_scalar(gsum[:], gsum[:], 1.0 / HC, None, ALU.mult))
                    if due(i):
                        dve.wait_ge(sq_ready, i)
                    nc.vector.tensor_tensor(cen[:], kv[:], spread(gsum[:]), ALU.subtract).then_inc(cen_ready, 1)
                    find_equal(dve, i, 1)
                    dve.wait_ge(sq_ready, i + 1)
                    step(nc.vector.tensor_reduce(gvar[:], sq[:], axis=AX.X, op=ALU.add))
                    nc.vector.tensor_scalar(gvar[:], gvar[:], 1.0 / HC, LN_EPS, ALU.mult, ALU.add)\
                      .then_inc(gvar_ready, 1)
                    dve.wait_ge(groot_ready, i + 1)
                    refine_rsqrt(nc, step, grstd[:], groot[:], gvar[:], gtmp[:])
                    if due(i):
                        dve.wait_ge(kv_prod, i)
                    step(nc.vector.tensor_tensor(kvn[:], cen[:], spread(grstd[:]), ALU.mult))
                    step(nc.vector.tensor_tensor(kvn[:], kvn[:], kv_g[:].rearrange("p s h c -> p (s h) c"),
                                                 ALU.mult))
                    nc.vector.tensor_tensor(kvn[:], kvn[:], kv_b[:].rearrange("p s h c -> p (s h) c"),
                                            ALU.add).then_inc(kvn_ready, 1)
                    dve.wait_ge(kv_prod, i + 1)
                    nc.vector.tensor_tensor(kvsum[:], kvsum[:],
                                            bank[4][:, 0:D].rearrange("p (k n) -> p k n", k=KD),
                                            ALU.add).then_inc(kv_added, 1)
                    dve.wait_ge(kv_added, i + 1)
                    assert done[0] == links

                first_apart(dve, H2, body)


            block = open_block()

            def view(b):
                return bank[b][:, 0:KD * C].rearrange("p (k n) -> p k n", k=KD)

            qp, rp, hp_, mp = view(3), view(4), view(5), view(6)

            @block.sync
            def _(sp):
                def body(i):
                    stage_group(sp, i + H2, 0)
                    stage_group(sp, i + H2, 1)

                first_apart(sp, 2 * NC, body)

            @block.gpsimd
            def _(pool):
                gather_group(pool, H2, 0)
                with pool.Fori(H2, H2 + 2 * NC - 1, 1) as h:
                    gather_group(pool, h, 1)
                    scatter_group(pool, h, 0)
                    gather_group(pool, h + 1, 0)
                    scatter_group(pool, h, 1)
                gather_group(pool, H2 + 2 * NC - 1, 1)
                scatter_group(pool, H2 + 2 * NC - 1, 0)
                scatter_group(pool, H2 + 2 * NC - 1, 1)
                for a in range(NA):
                    for g in range(2):
                        pool.wait_ge(scattered[a][g], 32 * (NG // 2))

            @block.tensor
            def _(pe):
                pe.wait_ge(attn_ready, 1)
                def body(i):
                    h = 2 * i + H2
                    at = bass.ds(i * C, C)

                    def product(to, w, xin):
                        for m in range(KD):
                            for k in range(KD):
                                last = nc.tensor.matmul(to[:, m, :], w(k, m), xin(k), start=k == 0, stop=k == KD - 1)
                        return last

                    turn_targets(pe, h, 0)
                    if due(2 * i):
                        pe.wait_ge(q_ready, 2 * i)
                    product(qp, lambda k, m: wq[:, k].rearrange("p h c -> p (h c)")[:, m * 128:(m + 1) * 128],
                            lambda k: U[:, k, at]).then_inc(q_made, 1)
                    turn_targets(pe, h, 1)
                    sum_equal(pe, h, 0)
                    pe.wait_ge(q_ready, 2 * i + 2)
                    if due(i):
                        pe.wait_ge(r_ready, i)
                    for m in range(KD):
                        last = nc.tensor.matmul(rp[:, m, :], attn[:, m, :], qs[:, m, :], start=True, stop=True)
                    last.then_inc(r_made, 1)
                    sum_equal(pe, h, 1)
                    turn_targets(pe, h + 1, 0)
                    turn_targets(pe, h + 1, 1)
                    pe.wait_ge(r_ready, i + 1)
                    if due(2 * i):
                        pe.wait_ge(h_ready, 2 * i)
                    product(hp_, lambda k, m: w1[:, k, m * 128:(m + 1) * 128], lambda k: rt[:, k, :]).then_inc(h_made, 1)
                    sum_equal(pe, h + 1, 0)
                    pe.wait_ge(h_ready, 2 * i + 2)
                    if due(2 * i):
                        pe.wait_ge(m_added, 2 * i)
                    product(mp, lambda k, m: w2[:, k, m * 128:(m + 1) * 128], lambda k: hm[:, k, :]).then_inc(m_made, 1)
                    sum_equal(pe, h + 1, 1)

                first_apart(pe, NC, body)

            @block.scalar
            def _(act):
                def body(i):
                    h = 2 * i + H2
                    act.wait_ge(q_made, i + 1)
                    if due(i):
                        act.wait_ge(r_made, i)
                    for m in range(KD):
                        nc.scalar.activation(qs[:, m, :], qp[:, m, :], ACT.Identity, bias=bq[:, m:m + 1])\
                          .then_inc(q_ready, 1)
                    copy_sums(act, h, 0)
                    copy_sums(act, h, 1)
                    act.wait_ge(h_made, i + 1)
                    if due(i):
                        act.wait_ge(m_made, i)
                    for m in range(KD):
                        nc.scalar.activation(hm[:, m, :], hp_[:, m, :], ACT.Gelu, bias=b1[:, m:m + 1])\
                          .then_inc(h_ready, 1)
                    copy_sums(act, h + 1, 0)
                    copy_sums(act, h + 1, 1)

                first_apart(act, NC, body)

            @block.vector
            def _(dve):
                nc.vector.memset(attn[:], 0.0).then_inc(attn0, 1)
                dve.wait_ge(attn0, 1)
                for s in range(4):
                    p = slice(32 * s, 32 * s + 32)
                    last = nc.vector.tensor_scalar(attn[p, :, p], kvsum[p, :, p], 1.0 / N, None, ALU.mult)
                last.then_inc(attn_ready, 1)
                def body(i):
                    h = 2 * i + H2
                    at = bass.ds(i * C, C)
                    cast_targets(dve, h, 0)
                    cast_targets(dve, h, 1)
                    find_equal(dve, h, 0)
                    find_equal(dve, h, 1)
                    dve.wait_ge(r_made, i + 1)
                    if due(i):
                        dve.wait_ge(h_made, i)
                    nc.vector.tensor_tensor(rt[:], rp, U[:, :, at], ALU.add).then_inc(r_ready, 1)
                    cast_targets(dve, h + 1, 0)
                    cast_targets(dve, h + 1, 1)
                    find_equal(dve, h + 1, 0)
                    find_equal(dve, h + 1, 1)
                    dve.wait_ge(m_made, i + 1)
                    for m in range(KD):
                        nc.vector.scalar_tensor_tensor(out=XT[:, m, at], in0=mp[:, m, :], scalar=b2[:, m:m + 1],
                                                       in1=XT[:, m, at], op0=ALU.add, op1=ALU.add)\
                          .then_inc(m_added, 1)

                first_apart(dve, NC, body)

        stage.close()

        with ExitStack() as st:
            gw1 = sb("gw1", [128, KD, FF], F32, st)
            gw2 = sb("gw2", [128, MF, D], F32, st)
            gbi1 = sb("gbi1", [128, MF], F32, st)
            gbi2 = sb("gbi2", [128, KD], F32, st)
            gam = sb("gam", [128, KD], F32, st)
            bet = sb("bet", [128, KD], F32, st)
            ht = sb("ht", [R, 2, NA, 2, D], F32, st)
            hsum = sb("hsum", [R, 2, 2, D], F32, st)
            hT = sb("hT", [128, KD, C], F32, st)
            hid = sb("hid", [128, MF, C], F32, st)
            bst = sb("bst", [128, KD, NC * 6], F32, st)
            bmv = sb("bmv", [128, KD, 2], F32, st)
            bscale = sb("bscale", [128, KD], F32, st)
            bvar, broot, btmp = (sb(n, [128, KD], F32, st) for n in ("bvar", "broot", "btmp"))
            gw_in, bvar_ready, broot_ready = sem("gw_in"), sem("bvar_ready"), sem("broot_ready")
            ht_in = [sem(f"ht_in{b}") for b in range(2)]
            hsum_ready, h_turned, hT_ready = sem("hsum_ready"), sem("h_turned"), sem("hT_ready")
            f_made, f_ready, o_made, o_ready, o_stats = (sem("f_made"), sem("f_ready"), sem("o_made"),
                                                         sem("o_ready"), sem("o_stats"))

            block = open_block()
            tview = bank[0][:, 0:KD * C].rearrange("p (k n) -> p k n", k=KD)
            fview = [bank[1 + m][:, 0:2 * C].rearrange("p (k n) -> p k n", k=2) for m in range(2)]
            oview = bank[3][:, 0:KD * C].rearrange("p (k n) -> p k n", k=KD)

            def chunks(engine, body, last=NC):
                body(0, 0, 0)
                body(1, 0, 1)
                with engine.Fori(1, last // 2, 1) as i:
                    body(2 * i, i, 0)
                    body(2 * i + 1, i, 1)
                if last % 2:
                    body(last - 1, last // 2, 0)

            @block.sync
            def _(sp):
                for to, v in ((gw1[:], gW1.rearrange("(k p) n -> p k n", p=128)),
                              (gw2[:], gW2.rearrange("(k p) n -> p k n", p=128)),
                              (gbi1[:], gb1.rearrange("(k p) -> p k", p=128)),
                              (gbi2[:], gb2.rearrange("(k p) -> p k", p=128)),
                              (gam[:], gamma.rearrange("(k p) -> p k", p=128)),
                              (bet[:], beta.rearrange("(k p) -> p k", p=128))):
                    sp.dma_start(to, v).then_inc(gw_in, 16)

                def body(c, n, b):
                    if due(2 * n):
                        sp.wait_ge(hsum_ready, 2 * n)
                    sp.sem_inc(sp_turn)
                    for a in range(NA):
                        rows_ = acc_d[a][bass.ds(c * C, C), :].rearrange("(j p) d -> p j d", p=R)
                        sp.dma_start(ht[:, b, a], rows_).then_inc(ht_in[b], 16)

                chunks(sp, body)

            @block.vector
            def _(dve):
                def body(c, n, b):
                    dve.wait_ge(ht_in[b], 16 * NA * (n + 1))
                    if due(2 * n):
                        dve.wait_ge(h_turned, 2 * n)
                    nc.vector.tensor_tensor(hsum[:, b], ht[:, b, 0], ht[:, b, 1], ALU.add).then_inc(hsum_ready, 1)

                def tail(c):
                    for m in range(KD):
                        dve.wait_ge(o_ready, 2 * c + m + 1)
                        nc.vector.bn_stats(bst[:, m, bass.ds(c * 6, 6)], U[:, m, bass.ds(c * C, C)])\
                          .then_inc(o_stats, 1)

                def pair(i):
                    body(2 * i, i, 0)
                    tail(2 * i)
                    body(2 * i + 1, i, 1)
                    tail(2 * i + 1)

                first_apart(dve, NC // 2, pair)
                body(NC - 1, NC // 2, 0)
                tail(NC - 1)
                dve.wait_ge(o_stats, 2 * NC)
                dve.wait_ge(gw_in, 16 * 6)
                for m in range(KD):
                    nc.vector.bn_aggr(bmv[:, m, :], bst[:, m, :]).then_inc(o_stats, 1)
                dve.wait_ge(o_stats, 2 * NC + 2)
                done = [2 * NC + 2]

                def step(ins):
                    done[0] += 1
                    ins.then_inc(o_stats, 1)
                    dve.wait_ge(o_stats, done[0])

                nc.vector.tensor_scalar(bvar[:], bmv[:, :, 1], LN_EPS, None, ALU.add).then_inc(bvar_ready, 1)
                dve.wait_ge(broot_ready, 1)
                refine_rsqrt(nc, step, bscale[:], broot[:], bvar[:], btmp[:])
                step(nc.vector.tensor_tensor(bscale[:], bscale[:], gam[:], ALU.mult))

            @block.tensor
            def _(pe):
                pe.wait_ge(gw_in, 16 * 6)

                def body(c, n, b):
                    pe.wait_ge(hsum_ready, c + 1)
                    if due(c):
                        pe.wait_ge(hT_ready, c)
                    for j in range(2):
                        for k in range(KD):
                            last = nc.tensor.transpose(tview[:, k, j * R:(j + 1) * R],
                                                       hsum[:, b, j, k * 128:(k + 1) * 128], ident[0:R, 0:R])
                    last.then_inc(h_turned, 1)
                    pe.wait_ge(hT_ready, c + 1)
                    if due(MF * c):
                        pe.wait_ge(f_ready, MF * c)
                    for m in range(MF):
                        for k in range(KD):
                            last = nc.tensor.matmul(fview[m // 2][:, m % 2, :], gw1[:, k, m * 128:(m + 1) * 128],
                                                    hT[:, k, :], start=k == 0, stop=k == KD - 1)
                        if m % 2:
                            last.then_inc(f_made, 1)
                    pe.wait_ge(f_ready, MF * (c + 1))
                    if due(KD * c):
                        pe.wait_ge(o_ready, KD * c)
                    for m in range(KD):
                        for k in range(MF):
                            last = nc.tensor.matmul(oview[:, m, :], gw2[:, k, m * 128:(m + 1) * 128], hid[:, k, :],
                                                    start=k == 0, stop=k == MF - 1)
                    last.then_inc(o_made, 1)

                chunks(pe, body)

            @block.scalar
            def _(act):
                def body(c, n, b):
                    act.wait_ge(h_turned, c + 1)
                    if due(2 * c):
                        act.wait_ge(f_made, 2 * c)
                    nc.scalar.activation(hT[:], tview, ACT.Copy).then_inc(hT_ready, 1)
                    if due(c):
                        act.wait_ge(o_made, c)
                    for m in range(MF):
                        act.wait_ge(f_made, 2 * c + m // 2 + 1)
                        nc.scalar.activation(hid[:, m, :], fview[m // 2][:, m % 2, :], ACT.Relu,
                                             bias=gbi1[:, m:m + 1]).then_inc(f_ready, 1)
                    act.wait_ge(o_made, c + 1)
                    for m in range(KD):
                        nc.scalar.activation(U[:, m, bass.ds(c * C, C)], oview[:, m, :], ACT.Identity,
                                             bias=gbi2[:, m:m + 1]).then_inc(o_ready, 1)

                act.wait_ge(gw_in, 16 * 6)
                chunks(act, body)
                act.wait_ge(bvar_ready, 1)
                nc.scalar.activation(broot[:], bvar[:], ACT.Sqrt).then_inc(broot_ready, 1)

            avg = sb("avg", [128, 128], F32, st)
            z = sb("z", [128, KD, C], F32, st)
            cent = sb("cent", [128, KD, C], F32, st)
            csq = sb("csq", [128, KD, C], F32, st)
            cvar, croot, crs, ctmp = (sb(n, [128, C], F32, st) for n in ("cvar", "croot", "crs", "ctmp"))
            xl = sb("xl", [128, KD, C], F32, st)
            res = sb("res", [128, KD, C], F32, st)
            x2 = sb("x2", [128, 2, C // B, KD, B, PARTS], BF16, st)
            avg_ready, z_ready, xt_ready, mean_made = sem("avg_ready"), sem("z_ready"), sem("xt_ready"), sem("mean_made")
            cent_ready, csq_ready, var_made = sem("cent_ready"), sem("csq_ready"), sem("var_made")
            rs_ready, xl_ready, p1_ready, r1_ready = sem("rs_ready"), sem("xl_ready"), sem("p1_ready"), sem("r1_ready")
            croot_ready, norm_chain = sem("croot_ready"), sem("norm_chain")
            p2_ready, p3_ready = sem("p2_ready"), sem("p3_ready")
            x2_out = [sem(f"x2_out{b}") for b in range(2)]
            CW = C // B * KD * B * PARTS

            block = open_block()

            def by_block(v):
                return v.rearrange("p k (n t) -> p k n t", t=B)

            def part(b, p):
                return x2[:, b, :, :, :, p].rearrange("p n k t -> p k n t")

            @block.tensor
            def _(pe):
                pe.wait_ge(avg_ready, 1)

                def body(c, n, b):
                    at = bass.ds(c * C, C)
                    pe.wait_ge(xt_ready, 2 * (c + 1))
                    if due(c):
                        pe.wait_ge(cent_ready, c)
                    for k in range(KD):
                        last = nc.tensor.matmul(bank[0][:, 0:C], avg[:], XT[:, k, at], start=k == 0, stop=k == KD - 1)
                    last.then_inc(mean_made, 1)
                    pe.wait_ge(csq_ready, c + 1)
                    if due(c):
                        pe.wait_ge(rs_ready, c)
                    for k in range(KD):
                        last = nc.tensor.matmul(bank[1][:, 0:C], avg[:], csq[:, k, :], start=k == 0, stop=k == KD - 1)
                    last.then_inc(var_made, 1)

                chunks(pe, body)

            @block.scalar
            def _(act):
                def body(c, n, b):
                    act.wait_ge(cent_ready, c + 1)
                    if due(c):
                        act.wait_ge(var_made, c)
                    nc.scalar.activation(csq[:], cent[:], ACT.Square).then_inc(csq_ready, 1)
                    act.wait_ge(rs_ready, c + 1)
                    nc.scalar.activation(croot[:], cvar[:], ACT.Sqrt).then_inc(croot_ready, 1)
                    act.wait_ge(xl_ready, c + 1)
                    if due(16 * n):
                        act.wait_ge(x2_out[b], 16 * n)
                    nc.scalar.activation(part(b, 0), by_block(xl[:]), ACT.Copy).then_inc(p1_ready, 1)
                    act.wait_ge(r1_ready, c + 1)
                    nc.scalar.activation(part(b, 1), by_block(res[:]), ACT.Copy).then_inc(p2_ready, 1)

                chunks(act, body)

            @block.vector
            def _(dve):
                nc.vector.memset(avg[:], 1.0 / D).then_inc(avg_ready, 1)

                def body(c, n, b):
                    at = bass.ds(c * C, C)
                    for m in range(KD):
                        nc.vector.tensor_scalar(z[:, m, :], U[:, m, at], bmv[:, m, 0:1], bscale[:, m:m + 1],
                                                ALU.subtract, ALU.mult).then_inc(z_ready, 1)
                    for m in range(KD):
                        dve.wait_ge(z_ready, 2 * c + m + 1)
                        nc.vector.scalar_tensor_tensor(out=XT[:, m, at], in0=z[:, m, :], scalar=bet[:, m:m + 1],
                                                       in1=XT[:, m, at], op0=ALU.add, op1=ALU.add)\
                          .then_inc(xt_ready, 1)
                    dve.wait_ge(xt_ready, 2 * c + 2)
                    dve.wait_ge(mean_made, c + 1)
                    if due(c):
                        dve.wait_ge(csq_ready, c)
                    mean = bank[0][:, 0:C].rearrange("p (o n) -> p o n", o=1).broadcast_to([128, KD, C])
                    nc.vector.tensor_tensor(cent[:], XT[:, :, at], mean, ALU.subtract).then_inc(cent_ready, 1)
                    dve.wait_ge(cent_ready, c + 1)
                    dve.wait_ge(var_made, c + 1)
                    nc.vector.tensor_scalar(cvar[:], bank[1][:, 0:C], LN_EPS, None, ALU.add).then_inc(rs_ready, 1)
                    dve.wait_ge(croot_ready, c + 1)
                    done = [0]

                    def step(ins):
                        done[0] += 1
                        ins.then_inc(norm_chain, 1)
                        dve.wait_ge(norm_chain, REFINE_STEPS * c + done[0])

                    refine_rsqrt(nc, step, crs[:], croot[:], cvar[:], ctmp[:])
                    if due(c):
                        dve.wait_ge(p1_ready, c)
                    rs2 = crs[:].rearrange("p (o n) -> p o n", o=1).broadcast_to([128, KD, C])
                    nc.vector.tensor_tensor(xl[:], cent[:], rs2, ALU.mult).then_inc(xl_ready, 1)
                    dve.wait_ge(xl_ready, c + 1)
                    dve.wait_ge(p1_ready, c + 1)
                    if due(c):
                        dve.wait_ge(p2_ready, c)
                    nc.vector.tensor_tensor(by_block(res[:]), by_block(xl[:]), part(b, 0), ALU.subtract)\
                      .then_inc(r1_ready, 1)
                    dve.wait_ge(r1_ready, c + 1)
                    dve.wait_ge(p2_ready, c + 1)
                    nc.vector.tensor_tensor(part(b, 2), by_block(res[:]), part(b, 1), ALU.subtract)\
                      .then_inc(p3_ready, 1)

                chunks(dve, body)

            @block.sync
            def _(sp):
                def body(c, n, b):
                    sp.wait_ge(p3_ready, c + 1)
                    sp.sem_inc(sp_turn)
                    sp.dma_start(x2_d[:, bass.ds(c * CW, CW)], x2[:, b].rearrange("p n k t c -> p (n k t c)"))\
                      .then_inc(x2_out[b], 16)

                chunks(sp, body)
                sp.wait_ge(x2_out[0], 16 * (NC - NC // 2))
                sp.wait_ge(x2_out[1], 16 * (NC // 2))

        stage.close()

        with ExitStack() as st:
            ones = sb("ones", [128, B], BF16, st)
            xs_ = sb("xsteps", [128, 2, KD, B, PARTS], BF16, st)
            hrest = sb("hrest", [128, PARTS, 2 * B, KD], F32, st)
            hpart = hrest[:].bitcast(BF16).rearrange("p c t (k e) -> p c t k e", e=2)[:, :, :, :, 1]
            gates = sb("gates", [128, 8], F32, st)
            og = sb("og", [128, 2], F32, st)
            first_tanh = sb("first_tanh", [128, 2], F32, st)
            uv = sb("uv", [128, 4], F32, st)
            gi = [bank[b][:, 0:B * IFG * 3].rearrange("p (t g c) -> p t g c", t=B, c=3) for b in range(2)]
            go = [bank[2 + b][:, 0:B * 2 * 3].rearrange("p (t g c) -> p t g c", t=B, c=3) for b in range(2)]
            zi, zo, tc = bank[4][:, 0:IFG], bank[5][:, 0:2], bank[6][:, 0:2]

            lstm0, tanh0, tanh_loaded = sem("lstm0"), sem("tanh0"), sem("tanh_loaded")
            xs_in = [sem(f"xs_in{b}") for b in range(2)]
            x_proj = sem("x_proj")
            h1_ready, h2_ready, h3_ready = sem("h1_ready"), sem("h2_ready"), sem("h3_ready")
            ifg_made, o_made_, ifg_summed, o_summed = (sem("ifg_made"), sem("ogate_made"), sem("ifg_summed"),
                                                       sem("ogate_summed"))
            ifg_act, o_act, uv_ready, c_ready, tc_ready = (
                sem("ifg_act"), sem("ogate_act"), sem("uv_ready"), sem("c_ready"), sem("tc_ready"))
            h_out = [sem(f"h_out{b}") for b in range(2)]
            XW = KD * B * PARTS

            block = open_block()

            def steps(engine, body):
                def blocks(i):
                    for b in range(2):
                        for s in range(B):
                            body(i * (2 * B) + (b * B + s), i, b, s)

                first_apart(engine, NI, blocks)

            @block.sync
            def _(sp):
                for b in range(2):
                    sp.dma_start(xs_[:, b].rearrange("p k t c -> p (k t c)"), x2_d[:, b * XW:(b + 1) * XW])\
                      .then_inc(xs_in[b], 16)
                with sp.Fori(0, NI, 1) as i:
                    for b in range(2):
                        sp.wait_ge(x_proj, 2 * i + b + 1)
                        sp.sem_inc(sp_turn)
                        sp.dma_start(xs_[:, b].rearrange("p k t c -> p (k t c)"),
                                     x2_d[:, bass.ds((2 * i + b + 2) * XW, XW)]).then_inc(xs_in[b], 16)
                        sp.wait_ge(h1_ready, (2 * i + b + 1) * B + 1)
                        sp.sem_inc(sp_turn)
                        sp.dma_start(Hs[:, bass.ds((2 * i + b) * B, B), :], hrest[:, 0, b * B:(b + 1) * B]).then_inc(h_out[b], 16)
                for b in range(2):
                    sp.wait_ge(h_out[b], 16 * NI)
                    sp.wait_ge(xs_in[b], 16 * (NI + 1))

            def projection(b):
                for g in range(GC):
                    to = gi[b][:, :, g, :] if g < IFG else go[b][:, :, g - IFG, :]
                    cols = slice(g * 128, (g + 1) * 128)
                    yield to[:, :, 0:1], gbias[:, cols], ones[:].rearrange("p (t c) -> p t c", c=1), g in (0, IFG)
                    for p in range(PARTS):
                        for k in range(KD):
                            yield to[:, :, 0:PARTS - p], wih[:, p, k, cols], xs_[:, b, k, :, 0:PARTS - p], False

            def matmul(to, w, v, start):
                return nc.tensor.matmul(to, w, v, start=start, stop=True, skip_group_check=True)

            @block.tensor
            def _(pe):
                pe.wait_ge(lstm0, 1)
                pe.wait_ge(xs_in[0], 16)
                for m in projection(0):
                    last = matmul(*m)
                last.then_inc(x_proj, 1)
                per_step = GC * (1 + PARTS * KD) // B
                state = {}

                def body(t, i, b, s):
                    if s == 0:
                        state["ahead"] = list(projection(1 - b))
                        pe.wait_ge(xs_in[1 - b], 16 * (i + 1 + b))
                    before = (b * B + s - 1) % (2 * B)
                    pe.wait_ge(h1_ready, t + 1)
                    for lo, n, to, made in ((0, IFG, gi[b], ifg_made), (IFG, 2, go[b], o_made_)):
                        for p in (2, 1, 0):
                            if lo == 0 and p == 1:
                                pe.wait_ge(h2_ready, t + 1)
                            if lo == 0 and p == 0:
                                pe.wait_ge(h3_ready, t + 1)
                            for g in range(n):
                                for k in range(KD):
                                    cols = slice((lo + g) * 128, (lo + g + 1) * 128)
                                    last = matmul(to[:, s, g, 0:PARTS - p], whh[:, p, k, cols],
                                                  hpart[:, 0:PARTS - p, before, k], False)
                        last.then_inc(made, 1)
                    n = per_step if s < B - 1 else len(state["ahead"])
                    for m in state["ahead"][:n]:
                        last = matmul(*m)
                    state["ahead"] = state["ahead"][n:]
                    if s == B - 1:
                        last.then_inc(x_proj, 1)

                steps(pe, body)

            @block.scalar
            def _(act):
                def body(t, i, b, s):
                    act.wait_ge(ifg_summed, t + 1)
                    nc.scalar.activation(gates[:, 0:IFG], zi, ACT.Tanh).then_inc(ifg_act, 1)
                    act.wait_ge(o_summed, t + 1)
                    nc.scalar.activation(og[:], zo, ACT.Tanh).then_inc(o_act, 1)
                    act.wait_ge(c_ready, t + 1)
                    nc.scalar.activation(tc, gates[:, 6:8], ACT.Tanh, scale=0.5).then_inc(tc_ready, 1)

                act.wait_ge(tanh0, 1)
                nc.scalar.activation(first_tanh[:], first_tanh[:], ACT.Tanh).then_inc(tanh_loaded, 1)
                steps(act, body)

            @block.vector
            def _(dve):
                nc.vector.memset(first_tanh[:], 0.0).then_inc(tanh0, 1)
                nc.vector.memset(ones[:], 1.0)
                nc.vector.memset(gates[:], 0.0)
                nc.vector.memset(hrest[:], 0.0).then_inc(lstm0, 1)
                dve.wait_ge(lstm0, 1)
                for s_ in (h1_ready, h2_ready, h3_ready):
                    dve.sem_inc(s_, 1)

                def body(t, i, b, s):
                    stt = nc.vector.scalar_tensor_tensor
                    dve.wait_ge(ifg_made, t + 1)
                    nc.vector.tensor_reduce(zi, gi[b][:, s], axis=AX.X, op=ALU.add).then_inc(ifg_summed, 1)
                    dve.wait_ge(ifg_act, t + 1)
                    stt(out=uv[:], in0=gates[:, 0:4], scalar=1.0, in1=gates[:, 4:8], op0=ALU.add, op1=ALU.mult)\
                        .then_inc(uv_ready, 1)
                    dve.wait_ge(o_made_, t + 1)
                    nc.vector.tensor_reduce(zo, go[b][:, s], axis=AX.X, op=ALU.add).then_inc(o_summed, 1)
                    dve.wait_ge(uv_ready, t + 1)
                    stt(out=gates[:, 6:8], in0=uv[:, 2:4], scalar=0.5, in1=uv[:, 0:2], op0=ALU.mult, op1=ALU.add)\
                        .then_inc(c_ready, 1)
                    dve.wait_ge(tc_ready, t + 1)
                    if s == 0 and due(16 * i):
                        dve.wait_ge(h_out[b], 16 * i)
                    at = b * B + s
                    stt(out=hrest[:, 0, at, :], in0=og[:], scalar=1.0, in1=tc, op0=ALU.add, op1=ALU.mult)\
                        .then_inc(h1_ready, 1)
                    dve.wait_ge(h1_ready, t + 2)
                    nc.vector.tensor_tensor(hrest[:, 1, at, :], hrest[:, 0, at, :], hpart[:, 0, at, :], ALU.subtract)\
                      .then_inc(h2_ready, 1)
                    dve.wait_ge(h2_ready, t + 2)
                    nc.vector.tensor_tensor(hrest[:, 2, at, :], hrest[:, 1, at, :], hpart[:, 1, at, :], ALU.subtract)\
                      .then_inc(h3_ready, 1)

                steps(dve, body)

        stage.close()

        with ExitStack() as st:
            wl = sb("wl", [128, KD, 2], F32, st)
            wlb = sb("wlb", [128, KD, 2, 128], F32, st)
            bl = sb("bl", [128, 2], F32, st)
            fw = sb("fw", [128, KD], F32, st)
            bw = sb("bw", [128, KD], F32, st)
            one = sb("one", [128, C], F32, st)
            inc = sb("inc", [128, KD, N], F32, st)
            l0 = sb("l0", [128, C], F32, st)
            gate = sb("gate", [128, C], F32, st)
            wgt = sb("wgt", [128, KD, C], F32, st)
            pre = sb("pre", [128, KD, C], F32, st)
            suf = sb("suf", [128, KD, C], F32, st)
            fin = sb("fin", [128, 2, KD, C], F32, st)
            ob = sb("ob", [R, 2, 2, D], F32, st)
            att_in, att_chain = sem("att_in"), sem("att_chain")
            l_made, l_used, g_ready, scan_done = sem("l_made"), sem("l_used"), sem("g_ready"), sem("scan_done")
            suf_ready, fin_ready, fin_turned, ob_ready = (sem("suf_ready"), sem("fin_ready"), sem("fin_turned"),
                                                          sem("ob_ready"))
            out_done = [sem(f"out_done{b}") for b in range(2)]
            wlb_ready = sem("wlb_ready")
            last_inc = sb("last_inc", [128, KD], F32, st)

            block = open_block()

            @block.sync
            def _(sp):
                for k in range(KD):
                    for l in range(2):
                        sp.dma_start(wl[:, k, l:l + 1], W_lin[l, k * 128:(k + 1) * 128].rearrange("(p o) -> p o", o=1))\
                          .then_inc(att_in, 16)
                sp.dma_start(bl[:], b_lin.rearrange("(a n) -> a n", a=1).broadcast_to([128, 2])).then_inc(att_in, 16)
                sp.dma_start(fw[:], fw_att.rearrange("o (k p) -> p (o k)", p=128)).then_inc(att_in, 16)
                sp.dma_start(bw[:], bw_att.rearrange("o (k p) -> p (o k)", p=128)).then_inc(att_in, 16)

                def body(c, n, b):
                    sp.wait_ge(ob_ready, c + 1)
                    sp.sem_inc(sp_turn)
                    sp.dma_start(out[bass.ds(c * C, C), :].rearrange("(j p) d -> p j d", p=R), ob[:, b])\
                      .then_inc(out_done[b], 16)

                chunks(sp, body)
                sp.wait_ge(out_done[0], 16 * (NC - NC // 2))
                sp.wait_ge(out_done[1], 16 * (NC // 2))

            @block.tensor
            def _(pe):
                pe.wait_ge(wlb_ready, 1)
                with pe.Fori(0, NC, 1) as c:
                    if due(2 * c):
                        pe.wait_ge(l_used, 2 * c)
                    for l in range(2):
                        for k in range(KD):
                            last = nc.tensor.matmul(bank[l][:, 0:C], wlb[:, k, l, :], Hs[:, bass.ds(c * C, C), k],
                                                    start=k == 0, stop=k == KD - 1)
                    last.then_inc(l_made, 1)

                def body(c, n, b):
                    pe.wait_ge(fin_ready, 2 * (c + 1))
                    if b:
                        pe.wait_ge(ob_ready, c - 1)
                    else:
                        if due(c):
                            pe.wait_ge(ob_ready, c)
                    for j in range(2):
                        for k in range(KD):
                            last = nc.tensor.transpose(bank[2 + b][0:R, j * D + k * 128:j * D + (k + 1) * 128],
                                                       fin[:, b, k, j * R:(j + 1) * R], ident[:])
                    last.then_inc(fin_turned, 1)

                chunks(pe, body)

            @block.scalar
            def _(act):
                def body(c, n, b):
                    act.wait_ge(fin_turned, c + 1)
                    if due(16 * n):
                        act.wait_ge(out_done[b], 16 * n)
                    nc.scalar.activation(ob[:, b].rearrange("p j d -> p (j d)"), bank[2 + b][0:R, :], ACT.Copy)\
                      .then_inc(ob_ready, 1)

                chunks(act, body)

            @block.vector
            def _(dve):
                stt = nc.vector.scalar_tensor_tensor
                nc.vector.memset(one[:], 1.0)
                dve.wait_ge(att_in, 16 * 7)
                nc.vector.tensor_scalar(fw[:], fw[:], 0.5, None, ALU.mult)
                nc.vector.tensor_scalar(bw[:], bw[:], 0.5, None, ALU.mult)
                nc.vector.tensor_scalar(wlb[:].rearrange("p k l n -> p (k l) n"),
                                        wl[:].rearrange("p k (l o) -> p (k l) o", o=1).broadcast_to([128, 2 * KD, 128]),
                                        0.5, None, ALU.mult).then_inc(wlb_ready, 1)
                dve.wait_ge(wlb_ready, 1)
                links = 8

                def forward(c, first):
                    done = [0]

                    def step(*instructions):
                        done[0] += 1
                        instructions[-1].then_inc(att_chain, 1)
                        dve.wait_ge(att_chain, links * c + done[0])

                    at = bass.ds(c * C, C)
                    hc = Hs[:, at, :].rearrange("p t k -> p k t")
                    dve.wait_ge(l_made, c + 1)
                    nc.vector.tensor_scalar(l0[:], bank[0][:, 0:C], bl[:, 0:1], None, ALU.add).then_inc(l_used, 1)
                    dve.wait_ge(l_used, 2 * c + 1)
                    stt(out=gate[:], in0=bank[1][:, 0:C], scalar=bl[:, 1:2], in1=l0[:], op0=ALU.add,
                        op1=ALU.is_gt).then_inc(l_used, 1)
                    dve.wait_ge(l_used, 2 * c + 2)
                    step(nc.vector.tensor_tensor(wgt[:], hc, gate[:].rearrange("p (o n) -> p o n", o=1)
                                                 .broadcast_to([128, KD, C]), ALU.mult))
                    for k in range(KD):
                        start = 0.0 if first else last_inc[:, k:k + 1]
                        step(nc.vector.tensor_tensor_scan(inc[:, k, at], one[:], wgt[:, k, :], start, ALU.mult,
                                                          ALU.add))
                    step(nc.vector.tensor_copy(last_inc[:].rearrange("p (k o) -> p k o", o=1),
                                               inc[:, :, bass.ds(c * C + (C - 1), 1)]))
                    step(nc.vector.tensor_tensor(pre[:], inc[:, :, at], wgt[:], ALU.subtract))
                    step(nc.vector.tensor_tensor(XT[:, :, at], XT[:, :, at], hc, ALU.add))
                    for k in range(KD):
                        step(stt(out=XT[:, k, at], in0=pre[:, k, :], scalar=fw[:, k:k + 1], in1=XT[:, k, at],
                                 op0=ALU.mult, op1=ALU.add))
                    assert done[0] == links

                forward(0, True)
                with dve.Fori(1, NC, 1) as c:
                    forward(c, False)

                def body(c, n, b):
                    at = bass.ds(c * C, C)
                    if due(2 * c):
                        dve.wait_ge(fin_ready, 2 * c)
                    for k in range(KD):
                        nc.vector.tensor_scalar(suf[:, k, :], inc[:, k, at], -1.0, last_inc[:, k:k + 1], ALU.mult,
                                                ALU.add).then_inc(suf_ready, 1)
                    if due(2 * n):
                        dve.wait_ge(fin_turned, 2 * n)
                    for k in range(KD):
                        dve.wait_ge(suf_ready, 2 * c + k + 1)
                        stt(out=fin[:, b, k, :], in0=suf[:, k, :], scalar=bw[:, k:k + 1], in1=XT[:, k, at],
                            op0=ALU.mult, op1=ALU.add).then_inc(fin_ready, 1)

                chunks(dve, body)


_INS = ["x", "src", "dst", "L0_gnn_eps", "L0_gnn_W1", "L0_gnn_b1", "L0_gnn_W2", "L0_gnn_b2", "L0_gnn_gamma",
        "L0_gnn_beta", "L0_mix_w_qkv", "L0_mix_b_qkv", "L0_mix_kln_g", "L0_mix_kln_b", "L0_mix_vln_g",
        "L0_mix_vln_b", "L0_mix_w1", "L0_mix_b1", "L0_mix_w2", "L0_mix_b2", "L0_ffn_W_ih", "L0_ffn_W_hh",
        "L0_ffn_b_ih", "L0_ffn_b_hh", "L0_ffn_W_lin", "L0_ffn_b_lin", "L0_ffn_fw_att", "L0_ffn_bw_att"]


def kernel(**inputs):
    import numpy as np
    import concourse.bacc as bacc
    from concourse.bass_utils import run_bass_kernel_spmd

    nc = bacc.Bacc("TRN2", target_bir_lowering=False, num_devices=1)
    arrays, args = {}, []
    for name in _INS:
        a = np.ascontiguousarray(inputs[name])
        arrays[f"in_{name}"] = a
        args.append(nc.dram_tensor(f"in_{name}", a.shape, mybir.dt.from_np(a.dtype), kind="ExternalInput").ap())
    args.append(nc.dram_tensor("out_x", (N, D), F32, kind="ExternalOutput").ap())
    gps_layer_kernel(nc, *args)
    r = run_bass_kernel_spmd(nc, [arrays], core_ids=[0])
    return r.results[0]["out_x"]
```

```python
from contextlib import ExitStack

import concourse.bass as bass
from concourse import mybir

F32 = mybir.dt.float32
BF16 = mybir.dt.bfloat16
I32 = mybir.dt.int32
ALU = mybir.AluOpType
ACT = mybir.ActivationFunctionType
AX = mybir.AxisListType

N, D, E = 6250, 256, 100000
KD = D // 128
R = 125
NT = N // R
C = 250
NC = N // C
XL = 5
HEADS, HC = 8, D // 8
FF = 2 * D
MF = FF // 128
GT = 4
NG = E // (R * GT)
NA = 2
G4 = 4 * D
GC = G4 // 128
IFG = 6
B = 5
NB = N // B
NI = NB // 2
PARTS = 3
LN_EPS = 1e-5
MIX_LOADS = 24


REFINE_STEPS = 5


def due(count):
    return not isinstance(count, int) or count > 0


def within(c):
    return not isinstance(c, int) or 0 <= c < NC


def first_apart(engine, steps, body):
    body(0)
    with engine.Fori(1, steps, 1) as i:
        body(i)


def refine_rsqrt(nc, step, y, root, v, t):
    step(nc.vector.reciprocal(y, root))
    step(nc.vector.tensor_tensor(t, y, y, ALU.mult))
    step(nc.vector.tensor_tensor(t, t, v, ALU.mult))
    step(nc.vector.tensor_scalar(t, t, -0.5, 1.5, ALU.mult, ALU.add))
    step(nc.vector.tensor_tensor(y, y, t, ALU.mult))


def gps_layer_kernel(nc, x, src, dst, gnn_eps, gW1, gb1, gW2, gb2, gamma, beta, w_qkv, b_qkv,
                     kln_g, kln_b, vln_g, vln_b, mw1, mb1, mw2, mb2, W_ih, W_hh, b_ih, b_hh,
                     W_lin, b_lin, fw_att, bw_att, out):
    xn_d = nc.dram_tensor("xn_d", (N, D), F32, kind="Internal").ap()
    acc_d = [nc.dram_tensor(f"acc{a}_d", (N + R, D), F32, kind="Internal").ap() for a in range(NA)]
    x2_d = nc.dram_tensor("x2_d", (128, (NB + 2) * KD * B * PARTS), BF16, kind="Internal").ap()

    top = ExitStack()
    stage = ExitStack()

    def open_block():
        stage.close()
        return stage.enter_context(nc.Block())

    with top, stage, nc.allow_non_contiguous_dma(reason="vectors of 256 numbers, loaded once"):
        def sem(name):
            return top.enter_context(nc.semaphore(name))

        def sb(name, shape, dt=F32, ctx=top):
            return ctx.enter_context(nc.sbuf_tensor(name, shape, dt))

        sp_turn, pool_turn = sem("sp_turn"), sem("pool_turn")

        bank = [top.enter_context(nc.psum_tensor(f"bank{i}", [128, 512], F32)) for i in range(8)]

        XT = sb("XT", [128, KD, N])
        U = sb("U", [128, KD, N])
        Hs = U[:, :, :].rearrange("p k n -> p (k n)").rearrange("p (t k) -> p t k", k=KD)
        whh = sb("whh", [128, PARTS, KD, G4], BF16)
        wih = sb("wih", [128, PARTS, KD, G4], BF16)
        gbias = sb("gbias", [128, G4], BF16)
        ident = sb("ident", [128, 128])
        kvsum = sb("kvsum", [128, KD, 128])

        stage.close()

        with ExitStack() as st:
            scratch = U[:, :, :].rearrange("p k n -> p (k n)")
            wraw = [scratch[:, w * GC * D:(w + 1) * GC * D].rearrange("p (c d) -> p c d", c=GC) for w in range(2)]
            wT = scratch[:, 4096:5120].rearrange("p (u n) -> p u n", u=2)
            wres = scratch[:, 5120:5632]
            brow = scratch[0:1, 5632:5632 + 2 * G4].rearrange("p (a n) -> p a n", a=2)
            bres = scratch[0:1, 7680:7680 + G4]
            ZW = (N + R) * D // R // 8
            zero = sb("zero", [R, ZW], F32, st)
            zero16 = sb("zero16", [128, 2 * KD * B * PARTS], BF16, st)
            one_eps = sb("one_eps", [R, 1], F32, st)
            xall = sb("xall", [R, NT, D], F32, st)
            xn = sb("xn", [R, 2, D], F32, st)
            a0 = sb("a0", [R, 2, D], F32, st)
            xs = sb("xs", [R, 2, D], F32, st)
            stats = sb("stats", [R, NT, 6], F32, st)
            mv = sb("mv", [R, NT, 2], F32, st)
            var = sb("var", [R, NT], F32, st)
            root = sb("root", [R, NT], F32, st)
            rstd = sb("rstd", [R, NT], F32, st)
            ntmp = sb("ntmp", [R, NT], F32, st)
            w_in, b_in, eps_in = sem("w_in"), sem("b_in"), sem("eps_in")
            x_in = [sem(f"x_in{j}") for j in range(XL)]
            var_ready, root_ready = sem("var_ready"), sem("root_ready")
            zeroed, ident0, ident_ready = sem("zeroed"), sem("ident0"), sem("ident_ready")
            zero_out = sem("zero_out")
            xn_out = [sem(f"xn_out{b}") for b in range(2)]
            w_turned, w_scaled, w_split = sem("w_turned"), sem("w_scaled"), sem("w_split")
            set_chain = sem("set_chain")
            xn_ready, xs_ready = sem("xn_ready"), sem("xs_ready")
            a0_ready = sem("a0_ready")
            x_turned, x_copied = sem("x_turned"), sem("x_copied")
            stats_made, mv_made = sem("stats_made"), sem("mv_made")

            SET_LINKS = 10 + 3 * 8 + REFINE_STEPS

            block = open_block()

            @block.sync
            def _(sp):
                xt = x.rearrange("(t p) d -> p t d", p=R)
                for j in range(XL):
                    at = slice(j * NT // XL, (j + 1) * NT // XL)
                    sp.dma_start(xall[:, at, :], xt[:, at, :]).then_inc(x_in[j], 16)
                for w, src_w in enumerate((W_hh, W_ih)):
                    sp.dma_start(wraw[w], src_w.rearrange("(c p) d -> p c d", p=128)).then_inc(w_in, 16)
                sp.dma_start(brow[:, 0, :], b_ih.rearrange("(a n) -> a n", a=1)).then_inc(b_in, 16)
                sp.dma_start(brow[:, 1, :], b_hh.rearrange("(a n) -> a n", a=1)).then_inc(b_in, 16)
                sp.dma_start(one_eps[:], gnn_eps.rearrange("(a n) -> a n", a=1).broadcast_to([R, 1])).then_inc(eps_in, 16)
                sp.wait_ge(zeroed, 2)
                flat = acc_d[1].rearrange("(p r) d -> p (r d)", p=R)
                for j in range(8):
                    sp.dma_start(flat[:, j * ZW:(j + 1) * ZW], zero[:]).then_inc(zero_out, 16)
                sp.dma_start(acc_d[0][N:N + R, :], zero[:, 0:D]).then_inc(zero_out, 16)
                sp.dma_start(x2_d[:, NB * KD * B * PARTS:], zero16[:]).then_inc(zero_out, 16)
                def body(i):
                    for b in range(2):
                        sp.wait_ge(a0_ready, 2 * i + b + 1)
                        sp.sem_inc(sp_turn)
                        sp.dma_start(xn_d[bass.ds((2 * i + b) * R, R), :], xn[:, b, :]).then_inc(xn_out[b], 16)
                        sp.dma_start(acc_d[0][bass.ds((2 * i + b) * R, R), :], a0[:, b, :]).then_inc(xn_out[b], 16)

                first_apart(sp, NT // 2, body)
                for b in range(2):
                    sp.wait_ge(xn_out[b], 32 * (NT // 2))
                sp.wait_ge(zero_out, 16 * 10)

            @block.gpsimd
            def _(pool):
                nc.gpsimd.memset(ident[:], 0.0).then_inc(ident0, 1)
                pool.wait_ge(ident0, 1)
                nc.gpsimd.affine_select(out=ident[:], in_=ident[:], compare_op=ALU.not_equal, fill=1.0, base=0,
                                        pattern=[[-1, 128]], channel_multiplier=1).then_inc(ident_ready, 1)

            @block.tensor
            def _(pe):
                pe.wait_ge(w_in, 32)
                pe.wait_ge(ident_ready, 1)
                for u in range(8):
                    w, k, half = u // 4, u // 2 % 2, u % 2
                    if u >= 2:
                        pe.wait_ge(w_scaled, u - 1)
                    for j in range(4):
                        last = nc.tensor.transpose(bank[u % 2][:, j * 128:(j + 1) * 128],
                                                   wraw[w][:, 4 * half + j, k * 128:(k + 1) * 128], ident[:])
                    last.then_inc(w_turned, 1)
                def body(i):
                    for b in range(2):
                        pe.wait_ge(xs_ready, 2 * i + b + 1)
                        if due(2 * (2 * i + b)):
                            pe.wait_ge(x_copied, 2 * (2 * i + b))
                        for k in range(KD):
                            nc.tensor.transpose(bank[2][:, k * R:(k + 1) * R], xn[:, b, k * 128:(k + 1) * 128],
                                                ident[0:R, 0:R])
                        for k in range(KD):
                            last = nc.tensor.transpose(bank[3][:, k * R:(k + 1) * R],
                                                       xs[:, b, k * 128:(k + 1) * 128], ident[0:R, 0:R])
                        last.then_inc(x_turned, 1)

                first_apart(pe, NT // 2, body)

            @block.scalar
            def _(act):
                for u in range(8):
                    w, half = u // 4, u % 2
                    s = 0.5 if w == 0 else 1.0
                    act.wait_ge(w_turned, u + 1)
                    if u >= 2:
                        act.wait_ge(w_split, u - 1)
                    for lo, hi, f in ((0, 256, 0.5 if half == 0 else 1.0), (256, 512, 0.5)):
                        last = nc.scalar.activation(wT[:, u % 2, lo:hi], bank[u % 2][:, lo:hi], ACT.Copy, scale=f * s)
                    last.then_inc(w_scaled, 1)
                act.wait_ge(var_ready, 1)
                nc.scalar.activation(root[:], var[:], ACT.Sqrt).then_inc(root_ready, 1)
                act.wait_ge(w_split, 8)
                act.wait_ge(set_chain, SET_LINKS)
                def body(i):
                    for b in range(2):
                        act.wait_ge(x_turned, 2 * i + b + 1)
                        at = bass.ds((2 * i + b) * R, R)
                        nc.scalar.activation(U[:, :, at], bank[2][:, 0:KD * R].rearrange("p (k n) -> p k n", k=KD),
                                             ACT.Copy).then_inc(x_copied, 1)
                        nc.scalar.activation(XT[:, :, at], bank[3][:, 0:KD * R].rearrange("p (k n) -> p k n", k=KD),
                                             ACT.Copy).then_inc(x_copied, 1)

                first_apart(act, NT // 2, body)

            @block.vector
            def _(dve):
                nc.vector.memset(zero[:], 0.0).then_inc(zeroed, 1)
                nc.vector.memset(zero16[:], 0.0).then_inc(zeroed, 1)
                count = [0]

                def link(ins):
                    count[0] += 1
                    ins.then_inc(set_chain, 1)
                    dve.wait_ge(set_chain, count[0])

                link(nc.vector.memset(gbias[:], 0.0))
                dve.wait_ge(b_in, 32)
                link(nc.vector.tensor_tensor(brow[:, 0, :], brow[:, 0, :], brow[:, 1, :], ALU.add))
                link(nc.vector.tensor_scalar(brow[:, 0, 0:2 * D], brow[:, 0, 0:2 * D], 0.5, None, ALU.mult))
                link(nc.vector.tensor_scalar(brow[:, 0, 3 * D:], brow[:, 0, 3 * D:], 0.5, None, ALU.mult))
                link(nc.vector.tensor_copy(gbias[0:1, :], brow[:, 0, :]))
                link(nc.vector.tensor_tensor(bres, brow[:, 0, :], gbias[0:1, :], ALU.subtract))
                link(nc.vector.tensor_copy(gbias[32:33, :], bres))
                link(nc.vector.tensor_copy(brow[:, 1, :], gbias[32:33, :]))
                link(nc.vector.tensor_tensor(gbias[64:65, :], bres, brow[:, 1, :], ALU.subtract))
                dve.wait_ge(eps_in, 16)
                link(nc.vector.tensor_scalar(one_eps[:], one_eps[:], 1.0, None, ALU.add))
                for u in range(8):
                    w, k, half = u // 4, u // 2 % 2, u % 2
                    parts = [(whh, wih)[w][:, p, k, half * 512:(half + 1) * 512] for p in range(PARTS)]
                    dve.wait_ge(w_scaled, u + 1)
                    link(nc.vector.tensor_copy(parts[0], wT[:, u % 2, :]))
                    link(nc.vector.tensor_tensor(wres, wT[:, u % 2, :], parts[0], ALU.subtract))
                    link(nc.vector.tensor_copy(parts[1], wres))
                    nc.vector.tensor_tensor(parts[2], wres, parts[1], ALU.subtract).then_inc(w_split, 1)
                dve.wait_ge(w_split, 8)
                for j in range(XL):
                    dve.wait_ge(x_in[j], 16)
                with dve.Fori(0, NT, 1) as t:
                    nc.vector.bn_stats(stats[:, bass.ds(t, 1), :].rearrange("p t s -> p (t s)"),
                                       xall[:, bass.ds(t, 1), :].rearrange("p t d -> p (t d)")).then_inc(stats_made, 1)
                dve.wait_ge(stats_made, NT)
                for t in range(NT):
                    nc.vector.bn_aggr(mv[:, t, :], stats[:, t, :]).then_inc(mv_made, 1)
                dve.wait_ge(mv_made, NT)
                nc.vector.tensor_scalar(var[:], mv[:, :, 1], LN_EPS, None, ALU.add).then_inc(var_ready, 1)
                dve.wait_ge(var_ready, 1)
                dve.wait_ge(root_ready, 1)
                refine_rsqrt(nc, link, rstd[:], root[:], var[:], ntmp[:])
                assert count[0] == SET_LINKS
                def body(i):
                    for b in range(2):
                        t = 2 * i + b
                        tile = xall[:, bass.ds(t, 1), :].rearrange("p t d -> p (t d)")
                        if due(32 * i):
                            dve.wait_ge(xn_out[b], 32 * i)
                        if b == 0:
                            if due(2 * i):
                                dve.wait_ge(x_turned, 2 * i)
                        mean = mv[:, bass.ds(t, 1), 0:1].rearrange("p t o -> p (t o)")
                        nc.vector.tensor_scalar(xn[:, b, :], tile, mean, rstd[:, bass.ds(t, 1)], ALU.subtract,
                                                ALU.mult).then_inc(xn_ready, 1)
                        dve.wait_ge(xn_ready, t + 1)
                        nc.vector.tensor_tensor(xs[:, b, :], tile, xn[:, b, :], ALU.add).then_inc(xs_ready, 1)
                        nc.vector.tensor_scalar(a0[:, b, :], xn[:, b, :], one_eps[:], None,
                                                ALU.mult).then_inc(a0_ready, 1)

                first_apart(dve, NT // 2, body)

        stage.close()

        with ExitStack() as st:
            staged_i = sb("staged_i", [R, 2, 2, GT], I32, st)
            dstf = sb("dstf", [R, 2, GT], F32, st)
            equal = sb("equal", [R, 2, GT, R], F32, st)
            earlier = sb("earlier", [R, GT, R], F32, st)
            below = sb("below", [R, R], F32, st)
            spare_i = sb("spare_i", [R, 1], I32, st)
            spare = sb("spare", [R, 1], F32, st)
            dup = sb("dup", [R, GT], F32, st)
            move = sb("move", [R, GT], F32, st)
            target = sb("target", [R, 2, GT], I32, st)
            rows = sb("rows", [R, 2, GT, D], F32, st)
            sums = sb("sums", [R, 2, GT, D], F32, st)

            wq = sb("wq", [128, KD, HEADS, HC], F32, st)
            wkv = sb("wkv", [128, KD, 2, HEADS, HC], F32, st)
            bq = sb("bq", [128, KD], F32, st)
            bkv = sb("bkv", [R, 2, HEADS, HC], F32, st)
            kv_g = sb("kv_g", [R, 2, HEADS, HC], F32, st)
            kv_b = sb("kv_b", [R, 2, HEADS, HC], F32, st)
            w1 = sb("w1", [128, KD, D], F32, st)
            w2 = sb("w2", [128, KD, D], F32, st)
            b1 = sb("b1", [128, KD], F32, st)
            b2 = sb("b2", [128, KD], F32, st)
            xk = sb("xk", [128, KD, R], F32, st)
            kv = sb("kv", [R, 2 * HEADS, HC], F32, st)
            cen = sb("cen", [R, 2 * HEADS, HC], F32, st)
            sq = sb("sq", [R, 2 * HEADS, HC], F32, st)
            gsum = sb("gsum", [R, 2 * HEADS], F32, st)
            gvar, groot, grstd, gtmp = (sb(n, [R, 2 * HEADS], F32, st) for n in ("gvar", "groot", "grstd", "gtmp"))
            kvn = sb("kvn", [R, 2 * HEADS, HC], F32, st)
            attn = sb("attn", [128, KD, 128], F32, st)
            qs = sb("qs", [128, KD, C], F32, st)
            rt = sb("rt", [128, KD, C], F32, st)
            hm = sb("hm", [128, KD, C], F32, st)

            staged = [sem(f"staged{g}") for g in range(2)]
            gathered = [sem(f"gathered{g}") for g in range(2)]
            scattered = [[sem(f"scattered{a}_{g}") for g in range(2)] for a in range(NA)]
            cast, dst_turned = sem("cast"), sem("dst_turned")
            equal_ready, target_ready = sem("equal_ready"), sem("target_ready")
            summed, sums_copied = sem("summed"), sem("sums_copied")
            edge_chain = sem("edge_chain")
            below0, below1, spare0, spare1 = sem("below0"), sem("below1"), sem("spare0"), sem("spare1")
            mixw_in, kv_chain = sem("mixw_in"), sem("kv_chain")
            xk_in, kv_made, kv_read = sem("xk_in"), sem("kv_made"), sem("kv_read")
            cen_ready, sq_ready, kvn_ready = sem("cen_ready"), sem("sq_ready"), sem("kvn_ready")
            gvar_ready, groot_ready = sem("gvar_ready"), sem("groot_ready")
            kv_prod, kv_added, kvsum0 = sem("kv_prod"), sem("kv_added"), sem("kvsum0")
            attn0, attn_ready = sem("attn0"), sem("attn_ready")
            q_made, q_ready, r_made, r_ready = sem("q_made"), sem("q_ready"), sem("r_made"), sem("r_ready")
            h_made, h_ready, m_made, m_added = sem("h_made"), sem("h_ready"), sem("m_made"), sem("m_added")

            turned = bank[0][0:R, 0:GT * R].rearrange("p (t n) -> p t n", t=GT)
            prod = [bank[1 + m][0:R, :].rearrange("p (t d) -> p t d", t=2) for m in range(2)]
            src_g = src.rearrange("(q p t) -> q p t", p=R, t=GT)
            dst_g = dst.rearrange("(q p t) -> q p t", p=R, t=GT)

            def stage_group(sp, h, g):
                if due(16 * GT * h):
                    sp.wait_ge(gathered[g], 16 * GT * h)
                sp.sem_inc(sp_turn)
                if due(2 * h):
                    sp.wait_ge(cast, 2 * h)
                sp.sem_inc(sp_turn)
                for s, v in enumerate((src_g, dst_g)):
                    sp.dma_start(staged_i[:, g, s, :], v[bass.ds(2 * h + g, 1)].rearrange("q p t -> p (q t)"))\
                      .then_inc(staged[g], 16)

            def gather_group(pool, h, g, first=False):
                pool.wait_ge(staged[g], 32 * (h + 1))
                if not first and due(2 * h + g - 1):
                    pool.wait_ge(summed, 2 * h + g - 1)
                    pool.sem_inc(pool_turn)
                for j in range(GT):
                    pool.indirect_dma_start(
                        out=rows[:, g, j, :], out_offset=None, in_=xn_d,
                        in_offset=bass.IndirectOffsetOnAxis(ap=staged_i[:, g, 0, j:j + 1], axis=0),
                    ).then_inc(gathered[g], 16)

            def scatter_group(pool, h, g):
                pool.wait_ge(target_ready, 2 * h + g + 1)
                pool.wait_ge(sums_copied, 2 * (2 * h + g + 1))
                pool.sem_inc(pool_turn)
                for j in range(GT):
                    a = j % NA
                    if j >= NA:
                        pool.wait_ge(scattered[a][g], 32 * h + 16)
                        pool.sem_inc(pool_turn)
                    elif g:
                        pool.wait_ge(scattered[a][0], 32 * (h + 1))
                        pool.sem_inc(pool_turn)
                    else:
                        if due(32 * h):
                            pool.wait_ge(scattered[a][1], 32 * h)
                        pool.sem_inc(pool_turn)
                    pool.indirect_dma_start(
                        out=acc_d[a], out_offset=bass.IndirectOffsetOnAxis(ap=target[:, g, j:j + 1], axis=0),
                        in_=sums[:, g, j, :], in_offset=None, compute_op=ALU.add,
                    ).then_inc(scattered[a][g], 16)

            def turn_targets(pe, h, g):
                pe.wait_ge(cast, 2 * h + g + 1)
                if due(2 * h + g):
                    pe.wait_ge(equal_ready, 2 * h + g)
                for j in range(GT):
                    last = nc.tensor.transpose(turned[:, j, :], dstf[:, g, j:j + 1].broadcast_to([R, R]),
                                               ident[0:R, 0:R])
                last.then_inc(dst_turned, 1)

            def sum_equal(pe, h, g):
                pe.wait_ge(equal_ready, 2 * h + g + 1)
                pe.wait_ge(gathered[g], 16 * GT * (h + 1))
                if due(2 * (2 * h + g)):
                    pe.wait_ge(sums_copied, 2 * (2 * h + g))
                for j in range(GT):
                    last = nc.tensor.matmul(prod[j // 2][:, j % 2, :], equal[:, g, j, :], rows[:, g, j, :],
                                            start=True, stop=True)
                last.then_inc(summed, 1)

            def copy_sums(act, h, g):
                act.wait_ge(summed, 2 * h + g + 1)
                for a in range(NA):
                    if due(32 * h):
                        act.wait_ge(scattered[a][g], 32 * h)
                for m in range(2):
                    nc.scalar.activation(sums[:, g, 2 * m:2 * m + 2, :], prod[m], ACT.Copy).then_inc(sums_copied, 1)

            EDGE_LINKS = 3

            def cast_targets(dve, h, g):
                dve.wait_ge(staged[g], 32 * (h + 1))
                if due(2 * h):
                    dve.wait_ge(target_ready, 2 * h)
                nc.vector.tensor_copy(dstf[:, g, :], staged_i[:, g, 1, :]).then_inc(cast, 1)

            def find_equal(dve, h, g):
                q = 2 * h + g
                done = [0]

                def step(ins):
                    done[0] += 1
                    ins.then_inc(edge_chain, 1)
                    dve.wait_ge(edge_chain, EDGE_LINKS * q + done[0])

                mine = dstf[:, g, :].rearrange("p (t o) -> p t o", o=1).broadcast_to([R, GT, R])
                dve.wait_ge(dst_turned, q + 1)
                if due(2 * h):
                    dve.wait_ge(summed, 2 * h)
                nc.vector.tensor_tensor(equal[:, g, :, :], turned, mine, ALU.is_equal).then_inc(equal_ready, 1)
                dve.wait_ge(equal_ready, q + 1)
                step(nc.vector.tensor_tensor(earlier[:], equal[:, g, :, :],
                                             below[:].rearrange("p (o n) -> p o n", o=1).broadcast_to([R, GT, R]),
                                             ALU.mult))
                step(nc.vector.tensor_reduce(dup[:], earlier[:], axis=AX.X, op=ALU.max))
                step(nc.vector.scalar_tensor_tensor(out=move[:], in0=dstf[:, g, :], scalar=spare[:], in1=dup[:],
                                                    op0=ALU.subtract, op1=ALU.mult))
                for a in range(NA):
                    if due(32 * h):
                        dve.wait_ge(scattered[a][g], 32 * h)
                nc.vector.tensor_tensor(target[:, g, :], dstf[:, g, :], move[:], ALU.subtract).then_inc(target_ready, 1)
                assert done[0] == EDGE_LINKS

            block = open_block()

            H2 = NT

            @block.sync
            def _(sp):
                ld = []
                wv = w_qkv.rearrange("(k p) (h s c) -> p k h s c", p=128, s=3, c=HC)
                for k in range(KD):
                    ld.append((wq[:, k], wv[:, k, :, 0, :]))
                    for s in range(2):
                        ld.append((wkv[:, k, s], wv[:, k, :, s + 1, :]))
                bv = b_qkv.rearrange("(h s c) -> s h c", s=3, c=HC)
                for k in range(KD):
                    for h in range(4):
                        ld.append((bq[32 * h:32 * h + 32, k:k + 1],
                                   bv[0, 4 * k + h, :].rearrange("(c o) -> c o", o=1)))
                for s in range(2):
                    ld.append((bkv[:, s], bv[s + 1:s + 2, :, :].broadcast_to([R, HEADS, HC])))
                for s, (g_, b_) in enumerate(((kln_g, kln_b), (vln_g, vln_b))):
                    for to, v in ((kv_g, g_), (kv_b, b_)):
                        ld.append((to[:, s], v.rearrange("(a o c) -> a o c", a=1, o=1).broadcast_to([R, HEADS, HC])))
                for to, v in ((w1, mw1), (w2, mw2)):
                    ld.append((to[:], v.rearrange("(k p) n -> p k n", p=128)))
                for to, v in ((b1, mb1), (b2, mb2)):
                    ld.append((to[:], v.rearrange("(k p) -> p k", p=128)))
                assert len(ld) == MIX_LOADS
                for to, v in ld:
                    sp.dma_start(to, v).then_inc(mixw_in, 16)
                def body(i):
                    stage_group(sp, i, 0)
                    stage_group(sp, i, 1)
                    if due(i):
                        sp.wait_ge(kv_made, i)
                    sp.sem_inc(sp_turn)
                    sp.dma_start(xk[:], U[:, :, bass.ds(i * R, R)]).then_inc(xk_in, 16)

                first_apart(sp, H2, body)

            @block.gpsimd
            def _(pool):
                nc.gpsimd.memset(below[:], 1.0).then_inc(below0, 1)
                nc.gpsimd.iota(spare_i[:], pattern=[[0, 1]], base=N, channel_multiplier=1).then_inc(spare0, 1)
                pool.wait_ge(below0, 1)
                nc.gpsimd.affine_select(out=below[:], in_=below[:], compare_op=ALU.is_ge, fill=0.0, base=-1,
                                        pattern=[[-1, R]], channel_multiplier=1).then_inc(below1, 1)
                gather_group(pool, 0, 0, first=True)
                def body(i):
                    gather_group(pool, i, 1)
                    scatter_group(pool, i, 0)
                    gather_group(pool, i + 1, 0)
                    scatter_group(pool, i, 1)

                first_apart(pool, H2 - 1, body)
                gather_group(pool, H2 - 1, 1)
                scatter_group(pool, H2 - 1, 0)
                scatter_group(pool, H2 - 1, 1)

            @block.tensor
            def _(pe):
                pe.wait_ge(mixw_in, 16 * MIX_LOADS)
                def body(i):
                    turn_targets(pe, i, 0)
                    pe.wait_ge(xk_in, 16 * (i + 1))
                    if due(i):
                        pe.wait_ge(kv_read, i)
                    for k in range(KD):
                        last = nc.tensor.matmul(bank[3][0:R, :], xk[:, k, :],
                                                wkv[:, k].rearrange("p s h c -> p (s h c)"),
                                                start=k == 0, stop=k == KD - 1)
                    last.then_inc(kv_made, 1)
                    turn_targets(pe, i, 1)
                    sum_equal(pe, i, 0)
                    pe.wait_ge(kvn_ready, i + 1)
                    if due(i):
                        pe.wait_ge(kv_added, i)
                    flat = kvn[:].rearrange("p s c -> p (s c)")
                    for c in range(KD):
                        last = nc.tensor.matmul(bank[4][:, c * 128:(c + 1) * 128], flat[:, c * 128:(c + 1) * 128],
                                                flat[:, D + c * 128:D + (c + 1) * 128], start=True, stop=True)
                    last.then_inc(kv_prod, 1)
                    sum_equal(pe, i, 1)

                first_apart(pe, H2, body)

            @block.scalar
            def _(act):
                def body(i):
                    act.wait_ge(cen_ready, i + 1)
                    nc.scalar.activation(sq[:], cen[:], ACT.Square).then_inc(sq_ready, 1)
                    copy_sums(act, i, 0)
                    act.wait_ge(gvar_ready, i + 1)
                    nc.scalar.activation(groot[:], gvar[:], ACT.Sqrt).then_inc(groot_ready, 1)
                    copy_sums(act, i, 1)

                first_apart(act, H2, body)

            @block.vector
            def _(dve):
                nc.vector.memset(kvsum[:], 0.0).then_inc(kvsum0, 1)
                dve.wait_ge(kvsum0, 1)
                dve.wait_ge(spare0, 1)
                dve.wait_ge(below1, 1)
                nc.vector.tensor_copy(spare[:], spare_i[:]).then_inc(spare1, 1)
                dve.wait_ge(spare1, 1)
                dve.wait_ge(mixw_in, 16 * MIX_LOADS)
                links = 5 + REFINE_STEPS
                def body(i):
                    done = [0]

                    def step(ins):
                        done[0] += 1
                        ins.then_inc(kv_chain, 1)
                        dve.wait_ge(kv_chain, links * i + done[0])

                    def spread(v):
                        return v.rearrange("p (s o) -> p s o", o=1).broadcast_to([R, 2 * HEADS, HC])

                    cast_targets(dve, i, 0)
                    cast_targets(dve, i, 1)
                    find_equal(dve, i, 0)
                    dve.wait_ge(kv_made, i + 1)
                    nc.vector.tensor_tensor(kv[:], bank[3][0:R, :].rearrange("p (s c) -> p s c", c=HC),
                                            bkv[:].rearrange("p s h c -> p (s h) c"), ALU.add).then_inc(kv_read, 1)
                    dve.wait_ge(kv_read, i + 1)
                    step(nc.vector.tensor_reduce(gsum[:], kv[:], axis=AX.X, op=ALU.add))
                    step(nc.vector.tensor_scalar(gsum[:], gsum[:], 1.0 / HC, None, ALU.mult))
                    if due(i):
                        dve.wait_ge(sq_ready, i)
                    nc.vector.tensor_tensor(cen[:], kv[:], spread(gsum[:]), ALU.subtract).then_inc(cen_ready, 1)
                    find_equal(dve, i, 1)
                    dve.wait_ge(sq_ready, i + 1)
                    step(nc.vector.tensor_reduce(gvar[:], sq[:], axis=AX.X, op=ALU.add))
                    nc.vector.tensor_scalar(gvar[:], gvar[:], 1.0 / HC, LN_EPS, ALU.mult, ALU.add)\
                      .then_inc(gvar_ready, 1)
                    dve.wait_ge(groot_ready, i + 1)
                    refine_rsqrt(nc, step, grstd[:], groot[:], gvar[:], gtmp[:])
                    if due(i):
                        dve.wait_ge(kv_prod, i)
                    step(nc.vector.tensor_tensor(kvn[:], cen[:], spread(grstd[:]), ALU.mult))
                    step(nc.vector.tensor_tensor(kvn[:], kvn[:], kv_g[:].rearrange("p s h c -> p (s h) c"),
                                                 ALU.mult))
                    nc.vector.tensor_tensor(kvn[:], kvn[:], kv_b[:].rearrange("p s h c -> p (s h) c"),
                                            ALU.add).then_inc(kvn_ready, 1)
                    dve.wait_ge(kv_prod, i + 1)
                    nc.vector.tensor_tensor(kvsum[:], kvsum[:],
                                            bank[4][:, 0:D].rearrange("p (k n) -> p k n", k=KD),
                                            ALU.add).then_inc(kv_added, 1)
                    dve.wait_ge(kv_added, i + 1)
                    assert done[0] == links

                first_apart(dve, H2, body)


            block = open_block()

            def view(b):
                return bank[b][:, 0:KD * C].rearrange("p (k n) -> p k n", k=KD)

            qp, rp, hp_, mp = view(3), view(4), view(5), view(6)

            @block.sync
            def _(sp):
                def body(i):
                    stage_group(sp, i + H2, 0)
                    stage_group(sp, i + H2, 1)

                first_apart(sp, 2 * NC, body)

            @block.gpsimd
            def _(pool):
                gather_group(pool, H2, 0)
                with pool.Fori(H2, H2 + 2 * NC - 1, 1) as h:
                    gather_group(pool, h, 1)
                    scatter_group(pool, h, 0)
                    gather_group(pool, h + 1, 0)
                    scatter_group(pool, h, 1)
                gather_group(pool, H2 + 2 * NC - 1, 1)
                scatter_group(pool, H2 + 2 * NC - 1, 0)
                scatter_group(pool, H2 + 2 * NC - 1, 1)
                for a in range(NA):
                    for g in range(2):
                        pool.wait_ge(scattered[a][g], 32 * (NG // 2))

            @block.tensor
            def _(pe):
                pe.wait_ge(attn_ready, 1)
                def body(i):
                    h = 2 * i + H2
                    at = bass.ds(i * C, C)

                    def product(to, w, xin):
                        for m in range(KD):
                            for k in range(KD):
                                last = nc.tensor.matmul(to[:, m, :], w(k, m), xin(k), start=k == 0, stop=k == KD - 1)
                        return last

                    turn_targets(pe, h, 0)
                    if due(2 * i):
                        pe.wait_ge(q_ready, 2 * i)
                    product(qp, lambda k, m: wq[:, k].rearrange("p h c -> p (h c)")[:, m * 128:(m + 1) * 128],
                            lambda k: U[:, k, at]).then_inc(q_made, 1)
                    turn_targets(pe, h, 1)
                    sum_equal(pe, h, 0)
                    pe.wait_ge(q_ready, 2 * i + 2)
                    if due(i):
                        pe.wait_ge(r_ready, i)
                    for m in range(KD):
                        last = nc.tensor.matmul(rp[:, m, :], attn[:, m, :], qs[:, m, :], start=True, stop=True)
                    last.then_inc(r_made, 1)
                    sum_equal(pe, h, 1)
                    turn_targets(pe, h + 1, 0)
                    turn_targets(pe, h + 1, 1)
                    pe.wait_ge(r_ready, i + 1)
                    if due(2 * i):
                        pe.wait_ge(h_ready, 2 * i)
                    product(hp_, lambda k, m: w1[:, k, m * 128:(m + 1) * 128], lambda k: rt[:, k, :]).then_inc(h_made, 1)
                    sum_equal(pe, h + 1, 0)
                    pe.wait_ge(h_ready, 2 * i + 2)
                    if due(2 * i):
                        pe.wait_ge(m_added, 2 * i)
                    product(mp, lambda k, m: w2[:, k, m * 128:(m + 1) * 128], lambda k: hm[:, k, :]).then_inc(m_made, 1)
                    sum_equal(pe, h + 1, 1)

                first_apart(pe, NC, body)

            @block.scalar
            def _(act):
                def body(i):
                    h = 2 * i + H2
                    act.wait_ge(q_made, i + 1)
                    if due(i):
                        act.wait_ge(r_made, i)
                    for m in range(KD):
                        nc.scalar.activation(qs[:, m, :], qp[:, m, :], ACT.Identity, bias=bq[:, m:m + 1])\
                          .then_inc(q_ready, 1)
                    copy_sums(act, h, 0)
                    copy_sums(act, h, 1)
                    act.wait_ge(h_made, i + 1)
                    if due(i):
                        act.wait_ge(m_made, i)
                    for m in range(KD):
                        nc.scalar.activation(hm[:, m, :], hp_[:, m, :], ACT.Gelu, bias=b1[:, m:m + 1])\
                          .then_inc(h_ready, 1)
                    copy_sums(act, h + 1, 0)
                    copy_sums(act, h + 1, 1)

                first_apart(act, NC, body)

            @block.vector
            def _(dve):
                nc.vector.memset(attn[:], 0.0).then_inc(attn0, 1)
                dve.wait_ge(attn0, 1)
                for s in range(4):
                    p = slice(32 * s, 32 * s + 32)
                    last = nc.vector.tensor_scalar(attn[p, :, p], kvsum[p, :, p], 1.0 / N, None, ALU.mult)
                last.then_inc(attn_ready, 1)
                def body(i):
                    h = 2 * i + H2
                    at = bass.ds(i * C, C)
                    cast_targets(dve, h, 0)
                    cast_targets(dve, h, 1)
                    find_equal(dve, h, 0)
                    find_equal(dve, h, 1)
                    dve.wait_ge(r_made, i + 1)
                    if due(i):
                        dve.wait_ge(h_made, i)
                    nc.vector.tensor_tensor(rt[:], rp, U[:, :, at], ALU.add).then_inc(r_ready, 1)
                    cast_targets(dve, h + 1, 0)
                    cast_targets(dve, h + 1, 1)
                    find_equal(dve, h + 1, 0)
                    find_equal(dve, h + 1, 1)
                    dve.wait_ge(m_made, i + 1)
                    for m in range(KD):
                        nc.vector.scalar_tensor_tensor(out=XT[:, m, at], in0=mp[:, m, :], scalar=b2[:, m:m + 1],
                                                       in1=XT[:, m, at], op0=ALU.add, op1=ALU.add)\
                          .then_inc(m_added, 1)

                first_apart(dve, NC, body)

        stage.close()

        with ExitStack() as st:
            gw1 = sb("gw1", [128, KD, FF], F32, st)
            gw2 = sb("gw2", [128, MF, D], F32, st)
            gbi1 = sb("gbi1", [128, MF], F32, st)
            gbi2 = sb("gbi2", [128, KD], F32, st)
            gam = sb("gam", [128, KD], F32, st)
            bet = sb("bet", [128, KD], F32, st)
            ht = sb("ht", [R, 2, NA, 2, D], F32, st)
            hsum = sb("hsum", [R, 2, 2, D], F32, st)
            hT = sb("hT", [128, KD, C], F32, st)
            hid = sb("hid", [128, 2, MF, C], F32, st)
            bst = sb("bst", [128, KD, NC * 6], F32, st)
            bmv = sb("bmv", [128, KD, 2], F32, st)
            bscale = sb("bscale", [128, KD], F32, st)
            bvar, broot, btmp, bshift = (sb(n, [128, KD], F32, st) for n in ("bvar", "broot", "btmp", "bshift"))
            gw_in, bvar_ready, broot_ready = sem("gw_in"), sem("bvar_ready"), sem("broot_ready")
            ht_in = [sem(f"ht_in{b}") for b in range(2)]
            hsum_ready, h_turned, hT_ready = sem("hsum_ready"), sem("h_turned"), sem("hT_ready")
            f_made, f_ready, o_made, o_ready, o_stats = (sem("f_made"), sem("f_ready"), sem("o_made"),
                                                         sem("o_ready"), sem("o_stats"))

            block = open_block()
            tview = bank[0][:, 0:KD * C].rearrange("p (k n) -> p k n", k=KD)
            fview = [bank[1 + m][:, 0:2 * C].rearrange("p (k n) -> p k n", k=2) for m in range(2)]
            oview = bank[3][:, 0:KD * C].rearrange("p (k n) -> p k n", k=KD)

            def chunks(engine, body, last=NC):
                body(0, 0, 0)
                body(1, 0, 1)
                with engine.Fori(1, last // 2, 1) as i:
                    body(2 * i, i, 0)
                    body(2 * i + 1, i, 1)
                if last % 2:
                    body(last - 1, last // 2, 0)

            @block.sync
            def _(sp):
                for to, v in ((gw1[:], gW1.rearrange("(k p) n -> p k n", p=128)),
                              (gw2[:], gW2.rearrange("(k p) n -> p k n", p=128)),
                              (gbi1[:], gb1.rearrange("(k p) -> p k", p=128)),
                              (gbi2[:], gb2.rearrange("(k p) -> p k", p=128)),
                              (gam[:], gamma.rearrange("(k p) -> p k", p=128)),
                              (bet[:], beta.rearrange("(k p) -> p k", p=128))):
                    sp.dma_start(to, v).then_inc(gw_in, 16)

                def body(c, n, b):
                    if due(2 * n):
                        sp.wait_ge(hsum_ready, 2 * n)
                    sp.sem_inc(sp_turn)
                    for a in range(NA):
                        rows_ = acc_d[a][bass.ds(c * C, C), :].rearrange("(j p) d -> p j d", p=R)
                        sp.dma_start(ht[:, b, a], rows_).then_inc(ht_in[b], 16)

                chunks(sp, body)

            @block.vector
            def _(dve):
                def sum_accumulators(c, n, b):
                    dve.wait_ge(ht_in[b], 16 * NA * (n + 1))
                    if due(2 * n):
                        dve.wait_ge(h_turned, 2 * n)
                    nc.vector.tensor_tensor(hsum[:, b], ht[:, b, 0], ht[:, b, 1], ALU.add).then_inc(hsum_ready, 1)

                def statistics(c):
                    for m in range(KD):
                        dve.wait_ge(o_ready, 2 * c + m + 1)
                        nc.vector.bn_stats(bst[:, m, bass.ds(c * 6, 6)], U[:, m, bass.ds(c * C, C)])\
                          .then_inc(o_stats, 1)

                def step(c, n, b):
                    if within(c + 1):
                        sum_accumulators(c + 1, n + b, 1 - b)
                    if within(c - 1):
                        statistics(c - 1)

                sum_accumulators(0, 0, 0)
                chunks(dve, step)
                statistics(NC - 1)
                dve.wait_ge(o_stats, 2 * NC)
                dve.wait_ge(gw_in, 16 * 6)
                for m in range(KD):
                    nc.vector.bn_aggr(bmv[:, m, :], bst[:, m, :]).then_inc(o_stats, 1)
                dve.wait_ge(o_stats, 2 * NC + 2)
                done = [2 * NC + 2]

                def step(ins):
                    done[0] += 1
                    ins.then_inc(o_stats, 1)
                    dve.wait_ge(o_stats, done[0])

                nc.vector.tensor_scalar(bvar[:], bmv[:, :, 1], LN_EPS, None, ALU.add).then_inc(bvar_ready, 1)
                dve.wait_ge(broot_ready, 1)
                refine_rsqrt(nc, step, bscale[:], broot[:], bvar[:], btmp[:])
                step(nc.vector.tensor_tensor(bscale[:], bscale[:], gam[:], ALU.mult))
                step(nc.vector.tensor_tensor(btmp[:], bscale[:], bmv[:, :, 0], ALU.mult))
                step(nc.vector.tensor_tensor(bshift[:], bet[:], btmp[:], ALU.subtract))

            @block.tensor
            def _(pe):
                pe.wait_ge(gw_in, 16 * 6)

                def turn(c, b):
                    pe.wait_ge(hsum_ready, c + 1)
                    if due(c):
                        pe.wait_ge(hT_ready, c)
                    for j in range(2):
                        for k in range(KD):
                            last = nc.tensor.transpose(tview[:, k, j * R:(j + 1) * R],
                                                       hsum[:, b, j, k * 128:(k + 1) * 128], ident[0:R, 0:R])
                    last.then_inc(h_turned, 1)

                def layer1(c):
                    pe.wait_ge(hT_ready, c + 1)
                    if due(MF * c):
                        pe.wait_ge(f_ready, MF * c)
                    for m in range(MF):
                        for k in range(KD):
                            last = nc.tensor.matmul(fview[m // 2][:, m % 2, :], gw1[:, k, m * 128:(m + 1) * 128],
                                                    hT[:, k, :], start=k == 0, stop=k == KD - 1)
                        if m % 2:
                            last.then_inc(f_made, 1)

                def layer2(c, b):
                    pe.wait_ge(f_ready, MF * (c + 1))
                    if due(KD * c):
                        pe.wait_ge(o_ready, KD * c)
                    for m in range(KD):
                        for k in range(MF):
                            last = nc.tensor.matmul(oview[:, m, :], gw2[:, k, m * 128:(m + 1) * 128],
                                                    hid[:, b, k, :], start=k == 0, stop=k == MF - 1)
                    last.then_inc(o_made, 1)

                def step(c, n, b):
                    layer1(c)
                    if within(c + 1):
                        turn(c + 1, 1 - b)
                    if within(c - 1):
                        layer2(c - 1, 1 - b)

                turn(0, 0)
                chunks(pe, step)
                layer2(NC - 1, (NC - 1) % 2)

            @block.scalar
            def _(act):
                def copy_turned(c):
                    act.wait_ge(h_turned, c + 1)
                    if due(2 * c):
                        act.wait_ge(f_made, 2 * c)
                    nc.scalar.activation(hT[:], tview, ACT.Copy).then_inc(hT_ready, 1)

                def hidden(c, b):
                    if due(c - 1):
                        act.wait_ge(o_made, c - 1)
                    for m in range(MF):
                        act.wait_ge(f_made, 2 * c + m // 2 + 1)
                        nc.scalar.activation(hid[:, b, m, :], fview[m // 2][:, m % 2, :], ACT.Relu,
                                             bias=gbi1[:, m:m + 1]).then_inc(f_ready, 1)

                def output(c):
                    act.wait_ge(o_made, c + 1)
                    for m in range(KD):
                        nc.scalar.activation(U[:, m, bass.ds(c * C, C)], oview[:, m, :], ACT.Identity,
                                             bias=gbi2[:, m:m + 1]).then_inc(o_ready, 1)

                def step(c, n, b):
                    hidden(c, b)
                    if within(c + 1):
                        copy_turned(c + 1)
                    if within(c - 1):
                        output(c - 1)

                act.wait_ge(gw_in, 16 * 6)
                copy_turned(0)
                chunks(act, step)
                output(NC - 1)
                act.wait_ge(bvar_ready, 1)
                nc.scalar.activation(broot[:], bvar[:], ACT.Sqrt).then_inc(broot_ready, 1)

            avg = sb("avg", [128, 128], F32, st)
            z = sb("z", [128, KD, C], F32, st)
            cent = sb("cent", [128, 2, KD, C], F32, st)
            csq = sb("csq", [128, KD, C], F32, st)
            cvar, croot, crs, ctmp = (sb(n, [128, C], F32, st) for n in ("cvar", "croot", "crs", "ctmp"))
            xl = sb("xl", [128, KD, C], F32, st)
            res = sb("res", [128, KD, C], F32, st)
            x2 = sb("x2", [128, 2, C // B, KD, B, PARTS], BF16, st)
            avg_ready, z_ready, xt_ready, mean_made = sem("avg_ready"), sem("z_ready"), sem("xt_ready"), sem("mean_made")
            cent_ready, csq_ready, var_made = sem("cent_ready"), sem("csq_ready"), sem("var_made")
            rs_ready, xl_ready, p1_ready, r1_ready = sem("rs_ready"), sem("xl_ready"), sem("p1_ready"), sem("r1_ready")
            croot_ready, norm_chain = sem("croot_ready"), sem("norm_chain")
            p2_ready, p3_ready = sem("p2_ready"), sem("p3_ready")
            x2_out = [sem(f"x2_out{b}") for b in range(2)]
            CW = C // B * KD * B * PARTS

            block = open_block()

            def by_block(v):
                return v.rearrange("p k (n t) -> p k n t", t=B)

            def part(b, p):
                return x2[:, b, :, :, :, p].rearrange("p n k t -> p k n t")

            def skewed(engine, step):
                for c in range(3):
                    step(c, c // 2, c % 2)
                with engine.Fori(1, (NC - 4) // 2, 1) as i:
                    step(2 * i + 1, i, 1)
                    step(2 * i + 2, i + 1, 0)
                for c in range((NC - 4) // 2 * 2 + 1, NC):
                    step(c, c // 2, c % 2)

            @block.tensor
            def _(pe):
                pe.wait_ge(avg_ready, 1)

                def mean(c, b):
                    at = bass.ds(c * C, C)
                    pe.wait_ge(xt_ready, c + 1)
                    if due(c - 1):
                        pe.wait_ge(cent_ready, c - 1)
                    for k in range(KD):
                        last = nc.tensor.matmul(bank[b][:, 0:C], avg[:], XT[:, k, at], start=k == 0, stop=k == KD - 1)
                    last.then_inc(mean_made, 1)

                def variance(c):
                    pe.wait_ge(csq_ready, c + 1)
                    if due(c):
                        pe.wait_ge(rs_ready, c)
                    for k in range(KD):
                        last = nc.tensor.matmul(bank[2][:, 0:C], avg[:], csq[:, k, :], start=k == 0, stop=k == KD - 1)
                    last.then_inc(var_made, 1)

                def step(c, n, b):
                    if within(c + 2):
                        mean(c + 2, b)
                    if within(c + 1):
                        variance(c + 1)

                mean(0, 0)
                mean(1, 1)
                variance(0)
                skewed(pe, step)

            @block.scalar
            def _(act):
                def batch_norm(c):
                    if due(c):
                        act.wait_ge(xt_ready, c)
                    for m in range(KD):
                        last = nc.scalar.activation(z[:, m, :], U[:, m, bass.ds(c * C, C)], ACT.Identity,
                                                    bias=bshift[:, m:m + 1], scale=bscale[:, m:m + 1])
                    last.then_inc(z_ready, 1)

                def square(c, b):
                    act.wait_ge(cent_ready, c + 1)
                    if due(c):
                        act.wait_ge(var_made, c)
                    nc.scalar.activation(csq[:], cent[:, b], ACT.Square).then_inc(csq_ready, 1)

                def second_part(c, b):
                    act.wait_ge(r1_ready, c + 1)
                    nc.scalar.activation(part(b, 1), by_block(res[:]), ACT.Copy).then_inc(p2_ready, 1)

                def step(c, n, b):
                    act.wait_ge(rs_ready, c + 1)
                    nc.scalar.activation(croot[:], cvar[:], ACT.Sqrt).then_inc(croot_ready, 1)
                    if within(c - 1):
                        second_part(c - 1, 1 - b)
                    if within(c + 1):
                        square(c + 1, 1 - b)
                    act.wait_ge(xl_ready, c + 1)
                    if due(16 * n):
                        act.wait_ge(x2_out[b], 16 * n)
                    nc.scalar.activation(part(b, 0), by_block(xl[:]), ACT.Copy).then_inc(p1_ready, 1)
                    if within(c + 3):
                        batch_norm(c + 3)

                batch_norm(0)
                batch_norm(1)
                square(0, 0)
                batch_norm(2)
                skewed(act, step)
                second_part(NC - 1, (NC - 1) % 2)

            @block.vector
            def _(dve):
                nc.vector.memset(avg[:], 1.0 / D).then_inc(avg_ready, 1)

                def residual(c):
                    at = bass.ds(c * C, C)
                    dve.wait_ge(z_ready, c + 1)
                    nc.vector.tensor_tensor(XT[:, :, at], XT[:, :, at], z[:], ALU.add).then_inc(xt_ready, 1)

                def center(c, b):
                    at = bass.ds(c * C, C)
                    mean = bank[b][:, 0:C].rearrange("p (o n) -> p o n", o=1).broadcast_to([128, KD, C])
                    dve.wait_ge(xt_ready, c + 1)
                    dve.wait_ge(mean_made, c + 1)
                    if due(c - 1):
                        dve.wait_ge(csq_ready, c - 1)
                        dve.wait_ge(xl_ready, c - 1)
                    nc.vector.tensor_tensor(cent[:, b], XT[:, :, at], mean, ALU.subtract).then_inc(cent_ready, 1)

                def first_rest(c, b):
                    dve.wait_ge(xl_ready, c + 1)
                    dve.wait_ge(p1_ready, c + 1)
                    if due(c):
                        dve.wait_ge(p2_ready, c)
                        dve.wait_ge(p3_ready, c)
                    nc.vector.tensor_tensor(by_block(res[:]), by_block(xl[:]), part(b, 0), ALU.subtract)\
                      .then_inc(r1_ready, 1)

                def third_part(c, b):
                    dve.wait_ge(r1_ready, c + 1)
                    dve.wait_ge(p2_ready, c + 1)
                    nc.vector.tensor_tensor(part(b, 2), by_block(res[:]), part(b, 1), ALU.subtract)\
                      .then_inc(p3_ready, 1)

                def step(c, n, b):
                    dve.wait_ge(var_made, c + 1)
                    nc.vector.tensor_scalar(cvar[:], bank[2][:, 0:C], LN_EPS, None, ALU.add).then_inc(rs_ready, 1)
                    if within(c + 2):
                        residual(c + 2)
                    if within(c - 1):
                        first_rest(c - 1, 1 - b)
                    if within(c + 1):
                        center(c + 1, 1 - b)
                    dve.wait_ge(rs_ready, c + 1)
                    dve.wait_ge(croot_ready, c + 1)
                    done = [0]

                    def link(ins):
                        done[0] += 1
                        ins.then_inc(norm_chain, 1)
                        dve.wait_ge(norm_chain, REFINE_STEPS * c + done[0])

                    refine_rsqrt(nc, link, crs[:], croot[:], cvar[:], ctmp[:])
                    if within(c - 1):
                        third_part(c - 1, 1 - b)
                    if due(c):
                        dve.wait_ge(p1_ready, c)
                        dve.wait_ge(r1_ready, c)
                    rs2 = crs[:].rearrange("p (o n) -> p o n", o=1).broadcast_to([128, KD, C])
                    nc.vector.tensor_tensor(xl[:], cent[:, b], rs2, ALU.mult).then_inc(xl_ready, 1)

                residual(0)
                residual(1)
                center(0, 0)
                skewed(dve, step)
                first_rest(NC - 1, (NC - 1) % 2)
                third_part(NC - 1, (NC - 1) % 2)

            @block.sync
            def _(sp):
                def body(c, n, b):
                    sp.wait_ge(p3_ready, c + 1)
                    sp.sem_inc(sp_turn)
                    sp.dma_start(x2_d[:, bass.ds(c * CW, CW)], x2[:, b].rearrange("p n k t c -> p (n k t c)"))\
                      .then_inc(x2_out[b], 16)

                chunks(sp, body)
                sp.wait_ge(x2_out[0], 16 * (NC - NC // 2))
                sp.wait_ge(x2_out[1], 16 * (NC // 2))

        stage.close()

        with ExitStack() as st:
            ones = sb("ones", [128, B], BF16, st)
            xs_ = sb("xsteps", [128, 2, KD, B, PARTS], BF16, st)
            hrest = sb("hrest", [128, PARTS, 2 * B, KD], F32, st)
            hpart = hrest[:].bitcast(BF16).rearrange("p c t (k e) -> p c t k e", e=2)[:, :, :, :, 1]
            gates = sb("gates", [128, 8], F32, st)
            og = sb("og", [128, 2], F32, st)
            first_tanh = sb("first_tanh", [128, 2], F32, st)
            uv = sb("uv", [128, 4], F32, st)
            gi = [bank[b][:, 0:B * IFG * 3].rearrange("p (t g c) -> p t g c", t=B, c=3) for b in range(2)]
            go = [bank[2 + b][:, 0:B * 2 * 3].rearrange("p (t g c) -> p t g c", t=B, c=3) for b in range(2)]
            zi, zo, tc = bank[4][:, 0:IFG], bank[5][:, 0:2], bank[6][:, 0:2]

            lstm0, tanh0, tanh_loaded = sem("lstm0"), sem("tanh0"), sem("tanh_loaded")
            xs_in = [sem(f"xs_in{b}") for b in range(2)]
            x_proj = sem("x_proj")
            h1_ready, h2_ready, h3_ready = sem("h1_ready"), sem("h2_ready"), sem("h3_ready")
            ifg_made, o_made_, ifg_summed, o_summed = (sem("ifg_made"), sem("ogate_made"), sem("ifg_summed"),
                                                       sem("ogate_summed"))
            ifg_act, o_act, uv_ready, c_ready, tc_ready = (
                sem("ifg_act"), sem("ogate_act"), sem("uv_ready"), sem("c_ready"), sem("tc_ready"))
            h_out = [sem(f"h_out{b}") for b in range(2)]
            XW = KD * B * PARTS

            block = open_block()

            def steps(engine, body):
                def blocks(i):
                    for b in range(2):
                        for s in range(B):
                            body(i * (2 * B) + (b * B + s), i, b, s)

                first_apart(engine, NI, blocks)

            @block.sync
            def _(sp):
                for b in range(2):
                    sp.dma_start(xs_[:, b].rearrange("p k t c -> p (k t c)"), x2_d[:, b * XW:(b + 1) * XW])\
                      .then_inc(xs_in[b], 16)
                with sp.Fori(0, NI, 1) as i:
                    for b in range(2):
                        sp.wait_ge(x_proj, 2 * i + b + 1)
                        sp.sem_inc(sp_turn)
                        sp.dma_start(xs_[:, b].rearrange("p k t c -> p (k t c)"),
                                     x2_d[:, bass.ds((2 * i + b + 2) * XW, XW)]).then_inc(xs_in[b], 16)
                        sp.wait_ge(h1_ready, (2 * i + b + 1) * B + 1)
                        sp.sem_inc(sp_turn)
                        sp.dma_start(Hs[:, bass.ds((2 * i + b) * B, B), :], hrest[:, 0, b * B:(b + 1) * B]).then_inc(h_out[b], 16)
                for b in range(2):
                    sp.wait_ge(h_out[b], 16 * NI)
                    sp.wait_ge(xs_in[b], 16 * (NI + 1))

            def projection(b):
                for g in range(GC):
                    to = gi[b][:, :, g, :] if g < IFG else go[b][:, :, g - IFG, :]
                    cols = slice(g * 128, (g + 1) * 128)
                    yield to[:, :, 0:1], gbias[:, cols], ones[:].rearrange("p (t c) -> p t c", c=1), g in (0, IFG)
                    for p in range(PARTS):
                        for k in range(KD):
                            yield to[:, :, 0:PARTS - p], wih[:, p, k, cols], xs_[:, b, k, :, 0:PARTS - p], False

            def matmul(to, w, v, start):
                return nc.tensor.matmul(to, w, v, start=start, stop=True, skip_group_check=True)

            @block.tensor
            def _(pe):
                pe.wait_ge(lstm0, 1)
                pe.wait_ge(xs_in[0], 16)
                for m in projection(0):
                    last = matmul(*m)
                last.then_inc(x_proj, 1)
                per_step = GC * (1 + PARTS * KD) // B
                state = {}

                def body(t, i, b, s):
                    if s == 0:
                        state["ahead"] = list(projection(1 - b))
                        pe.wait_ge(xs_in[1 - b], 16 * (i + 1 + b))
                    before = (b * B + s - 1) % (2 * B)
                    pe.wait_ge(h1_ready, t + 1)
                    for lo, n, to, made in ((0, IFG, gi[b], ifg_made), (IFG, 2, go[b], o_made_)):
                        for p in (2, 1, 0):
                            if lo == 0 and p == 1:
                                pe.wait_ge(h2_ready, t + 1)
                            if lo == 0 and p == 0:
                                pe.wait_ge(h3_ready, t + 1)
                            for g in range(n):
                                for k in range(KD):
                                    cols = slice((lo + g) * 128, (lo + g + 1) * 128)
                                    last = matmul(to[:, s, g, 0:PARTS - p], whh[:, p, k, cols],
                                                  hpart[:, 0:PARTS - p, before, k], False)
                        last.then_inc(made, 1)
                    n = per_step if s < B - 1 else len(state["ahead"])
                    for m in state["ahead"][:n]:
                        last = matmul(*m)
                    state["ahead"] = state["ahead"][n:]
                    if s == B - 1:
                        last.then_inc(x_proj, 1)

                steps(pe, body)

            @block.scalar
            def _(act):
                def body(t, i, b, s):
                    act.wait_ge(ifg_summed, t + 1)
                    nc.scalar.activation(gates[:, 0:IFG], zi, ACT.Tanh).then_inc(ifg_act, 1)
                    act.wait_ge(o_summed, t + 1)
                    nc.scalar.activation(og[:], zo, ACT.Tanh).then_inc(o_act, 1)
                    act.wait_ge(c_ready, t + 1)
                    nc.scalar.activation(tc, gates[:, 6:8], ACT.Tanh, scale=0.5).then_inc(tc_ready, 1)

                act.wait_ge(tanh0, 1)
                nc.scalar.activation(first_tanh[:], first_tanh[:], ACT.Tanh).then_inc(tanh_loaded, 1)
                steps(act, body)

            @block.vector
            def _(dve):
                nc.vector.memset(first_tanh[:], 0.0).then_inc(tanh0, 1)
                nc.vector.memset(ones[:], 1.0)
                nc.vector.memset(gates[:], 0.0)
                nc.vector.memset(hrest[:], 0.0).then_inc(lstm0, 1)
                dve.wait_ge(lstm0, 1)
                for s_ in (h1_ready, h2_ready, h3_ready):
                    dve.sem_inc(s_, 1)

                def body(t, i, b, s):
                    stt = nc.vector.scalar_tensor_tensor
                    dve.wait_ge(ifg_made, t + 1)
                    nc.vector.tensor_reduce(zi, gi[b][:, s], axis=AX.X, op=ALU.add).then_inc(ifg_summed, 1)
                    dve.wait_ge(ifg_act, t + 1)
                    stt(out=uv[:], in0=gates[:, 0:4], scalar=1.0, in1=gates[:, 4:8], op0=ALU.add, op1=ALU.mult)\
                        .then_inc(uv_ready, 1)
                    dve.wait_ge(o_made_, t + 1)
                    nc.vector.tensor_reduce(zo, go[b][:, s], axis=AX.X, op=ALU.add).then_inc(o_summed, 1)
                    dve.wait_ge(uv_ready, t + 1)
                    stt(out=gates[:, 6:8], in0=uv[:, 2:4], scalar=0.5, in1=uv[:, 0:2], op0=ALU.mult, op1=ALU.add)\
                        .then_inc(c_ready, 1)
                    dve.wait_ge(tc_ready, t + 1)
                    if s == 0 and due(16 * i):
                        dve.wait_ge(h_out[b], 16 * i)
                    at = b * B + s
                    stt(out=hrest[:, 0, at, :], in0=og[:], scalar=1.0, in1=tc, op0=ALU.add, op1=ALU.mult)\
                        .then_inc(h1_ready, 1)
                    dve.wait_ge(h1_ready, t + 2)
                    nc.vector.tensor_tensor(hrest[:, 1, at, :], hrest[:, 0, at, :], hpart[:, 0, at, :], ALU.subtract)\
                      .then_inc(h2_ready, 1)
                    dve.wait_ge(h2_ready, t + 2)
                    nc.vector.tensor_tensor(hrest[:, 2, at, :], hrest[:, 1, at, :], hpart[:, 1, at, :], ALU.subtract)\
                      .then_inc(h3_ready, 1)

                steps(dve, body)

        stage.close()

        with ExitStack() as st:
            wl = sb("wl", [128, KD, 2], F32, st)
            wlb = sb("wlb", [128, KD, 2, 128], F32, st)
            bl = sb("bl", [128, 2], F32, st)
            fw = sb("fw", [128, KD], F32, st)
            bw = sb("bw", [128, KD], F32, st)
            one = sb("one", [128, C], F32, st)
            inc = sb("inc", [128, KD, N], F32, st)
            l0 = sb("l0", [128, C], F32, st)
            gate = sb("gate", [128, C], F32, st)
            wgt = sb("wgt", [128, KD, C], F32, st)
            pre = sb("pre", [128, KD, C], F32, st)
            suf = sb("suf", [128, 2, KD, C], F32, st)
            fin = sb("fin", [128, 2, KD, C], F32, st)
            ob = sb("ob", [R, 2, 2, D], F32, st)
            att_in, fw_ready = sem("att_in"), sem("fw_ready")
            l_made, l0_ready, gate_ready, wgt_ready = sem("l_made"), sem("l0_ready"), sem("gate_ready"), sem("wgt_ready")
            scan_done, last_ready, pre_ready = sem("scan_done"), sem("last_ready"), sem("pre_ready")
            sum_ready, fwd_ready = sem("sum_ready"), sem("fwd_ready")
            suf_ready, fin_ready, fin_turned, ob_ready = (sem("suf_ready"), sem("fin_ready"), sem("fin_turned"),
                                                          sem("ob_ready"))
            out_done = [sem(f"out_done{b}") for b in range(2)]
            wlb_ready = sem("wlb_ready")
            last_inc = sb("last_inc", [128, KD], F32, st)

            block = open_block()

            @block.sync
            def _(sp):
                for k in range(KD):
                    for l in range(2):
                        sp.dma_start(wl[:, k, l:l + 1], W_lin[l, k * 128:(k + 1) * 128].rearrange("(p o) -> p o", o=1))\
                          .then_inc(att_in, 16)
                sp.dma_start(bl[:], b_lin.rearrange("(a n) -> a n", a=1).broadcast_to([128, 2])).then_inc(att_in, 16)
                sp.dma_start(fw[:], fw_att.rearrange("o (k p) -> p (o k)", p=128)).then_inc(att_in, 16)
                sp.dma_start(bw[:], bw_att.rearrange("o (k p) -> p (o k)", p=128)).then_inc(att_in, 16)

                def body(c, n, b):
                    sp.wait_ge(ob_ready, c + 1)
                    sp.sem_inc(sp_turn)
                    sp.dma_start(out[bass.ds(c * C, C), :].rearrange("(j p) d -> p j d", p=R), ob[:, b])\
                      .then_inc(out_done[b], 16)

                chunks(sp, body)
                sp.wait_ge(out_done[0], 16 * (NC - NC // 2))
                sp.wait_ge(out_done[1], 16 * (NC // 2))

            @block.tensor
            def _(pe):
                pe.wait_ge(wlb_ready, 1)

                def logits(c):
                    if due(c):
                        pe.wait_ge(l0_ready, c)
                        pe.wait_ge(gate_ready, c)
                    for l in range(2):
                        for k in range(KD):
                            last = nc.tensor.matmul(bank[l][:, 0:C], wlb[:, k, l, :], Hs[:, bass.ds(c * C, C), k],
                                                    start=k == 0, stop=k == KD - 1)
                    last.then_inc(l_made, 1)

                first_apart(pe, NC, logits)

                def body(c, n, b):
                    pe.wait_ge(fin_ready, 2 * (c + 1))
                    if b:
                        pe.wait_ge(ob_ready, c - 1)
                    else:
                        if due(c):
                            pe.wait_ge(ob_ready, c)
                    for j in range(2):
                        for k in range(KD):
                            last = nc.tensor.transpose(bank[2 + b][0:R, j * D + k * 128:j * D + (k + 1) * 128],
                                                       fin[:, b, k, j * R:(j + 1) * R], ident[:])
                    last.then_inc(fin_turned, 1)

                chunks(pe, body)

            @block.scalar
            def _(act):
                act.wait_ge(att_in, 16 * 7)

                def logit0(c):
                    act.wait_ge(l_made, c + 1)
                    if due(c):
                        act.wait_ge(gate_ready, c)
                    nc.scalar.activation(l0[:], bank[0][:, 0:C], ACT.Identity, bias=bl[:, 0:1]).then_inc(l0_ready, 1)

                first_apart(act, NC, logit0)

                def suffix(c, b):
                    if due(2 * (c - 1)):
                        act.wait_ge(fin_ready, 2 * (c - 1))
                    for k in range(KD):
                        nc.scalar.activation(suf[:, b, k, :], inc[:, k, bass.ds(c * C, C)], ACT.Identity, scale=-1.0,
                                             bias=last_inc[:, k:k + 1]).then_inc(suf_ready, 1)

                def body(c, n, b):
                    if within(c + 1):
                        suffix(c + 1, 1 - b)
                    act.wait_ge(fin_turned, c + 1)
                    if due(16 * n):
                        act.wait_ge(out_done[b], 16 * n)
                    nc.scalar.activation(ob[:, b].rearrange("p j d -> p (j d)"), bank[2 + b][0:R, :], ACT.Copy)\
                      .then_inc(ob_ready, 1)

                act.wait_ge(scan_done, 2 * NC)
                act.wait_ge(last_ready, NC)
                suffix(0, 0)
                chunks(act, body)

            @block.vector
            def _(dve):
                stt = nc.vector.scalar_tensor_tensor
                nc.vector.memset(one[:], 1.0)
                dve.wait_ge(att_in, 16 * 7)
                nc.vector.tensor_scalar(fw[:], fw[:], 0.5, None, ALU.mult)
                nc.vector.tensor_scalar(bw[:], bw[:], 0.5, None, ALU.mult).then_inc(fw_ready, 1)
                nc.vector.tensor_scalar(wlb[:].rearrange("p k l n -> p (k l) n"),
                                        wl[:].rearrange("p k (l o) -> p (k l) o", o=1).broadcast_to([128, 2 * KD, 128]),
                                        0.5, None, ALU.mult).then_inc(wlb_ready, 1)
                dve.wait_ge(wlb_ready, 1)
                dve.wait_ge(fw_ready, 1)

                def states(c):
                    return Hs[:, bass.ds(c * C, C), :].rearrange("p t k -> p k t")

                def choose(c):
                    dve.wait_ge(l_made, c + 1)
                    dve.wait_ge(l0_ready, c + 1)
                    if due(c):
                        dve.wait_ge(wgt_ready, c)
                    stt(out=gate[:], in0=bank[1][:, 0:C], scalar=bl[:, 1:2], in1=l0[:], op0=ALU.add,
                        op1=ALU.is_gt).then_inc(gate_ready, 1)

                def weigh(c):
                    dve.wait_ge(gate_ready, c + 1)
                    if due(c):
                        dve.wait_ge(scan_done, 2 * c)
                        dve.wait_ge(pre_ready, c)
                    nc.vector.tensor_tensor(wgt[:], states(c), gate[:].rearrange("p (o n) -> p o n", o=1)
                                            .broadcast_to([128, KD, C]), ALU.mult).then_inc(wgt_ready, 1)

                def forward(c, first=False, last=False):
                    at = bass.ds(c * C, C)
                    if not last:
                        choose(c + 1)
                    dve.wait_ge(wgt_ready, c + 1)
                    if not first:
                        dve.wait_ge(last_ready, c)
                    for k in range(KD):
                        start = 0.0 if first else last_inc[:, k:k + 1]
                        nc.vector.tensor_tensor_scan(inc[:, k, at], one[:], wgt[:, k, :], start, ALU.mult,
                                                     ALU.add).then_inc(scan_done, 1)
                    nc.vector.tensor_tensor(XT[:, :, at], XT[:, :, at], states(c), ALU.add).then_inc(sum_ready, 1)
                    dve.wait_ge(scan_done, 2 * c + 2)
                    if not first:
                        dve.wait_ge(fwd_ready, 2 * c)
                    nc.vector.tensor_tensor(pre[:], inc[:, :, at], wgt[:], ALU.subtract).then_inc(pre_ready, 1)
                    nc.vector.tensor_copy(last_inc[:].rearrange("p (k o) -> p k o", o=1),
                                          inc[:, :, bass.ds(c * C + (C - 1), 1)]).then_inc(last_ready, 1)
                    if not last:
                        weigh(c + 1)
                    dve.wait_ge(pre_ready, c + 1)
                    dve.wait_ge(sum_ready, c + 1)
                    for k in range(KD):
                        stt(out=XT[:, k, at], in0=pre[:, k, :], scalar=fw[:, k:k + 1], in1=XT[:, k, at],
                            op0=ALU.mult, op1=ALU.add).then_inc(fwd_ready, 1)

                choose(0)
                weigh(0)
                forward(0, first=True)
                with dve.Fori(1, NC - 1, 1) as c:
                    forward(c)
                forward(NC - 1, last=True)
                dve.wait_ge(fwd_ready, 2 * NC)

                def body(c, n, b):
                    at = bass.ds(c * C, C)
                    if due(n):
                        dve.wait_ge(fin_turned, c - 1)
                    for k in range(KD):
                        dve.wait_ge(suf_ready, 2 * c + k + 1)
                        stt(out=fin[:, b, k, :], in0=suf[:, b, k, :], scalar=bw[:, k:k + 1], in1=XT[:, k, at],
                            op0=ALU.mult, op1=ALU.add).then_inc(fin_ready, 1)

                chunks(dve, body)


_INS = ["x", "src", "dst", "L0_gnn_eps", "L0_gnn_W1", "L0_gnn_b1", "L0_gnn_W2", "L0_gnn_b2", "L0_gnn_gamma",
        "L0_gnn_beta", "L0_mix_w_qkv", "L0_mix_b_qkv", "L0_mix_kln_g", "L0_mix_kln_b", "L0_mix_vln_g",
        "L0_mix_vln_b", "L0_mix_w1", "L0_mix_b1", "L0_mix_w2", "L0_mix_b2", "L0_ffn_W_ih", "L0_ffn_W_hh",
        "L0_ffn_b_ih", "L0_ffn_b_hh", "L0_ffn_W_lin", "L0_ffn_b_lin", "L0_ffn_fw_att", "L0_ffn_bw_att"]


def kernel(**inputs):
    import numpy as np
    import concourse.bacc as bacc
    from concourse.bass_utils import run_bass_kernel_spmd

    nc = bacc.Bacc("TRN2", target_bir_lowering=False, num_devices=1)
    arrays, args = {}, []
    for name in _INS:
        a = np.ascontiguousarray(inputs[name])
        arrays[f"in_{name}"] = a
        args.append(nc.dram_tensor(f"in_{name}", a.shape, mybir.dt.from_np(a.dtype), kind="ExternalInput").ap())
    args.append(nc.dram_tensor("out_x", (N, D), F32, kind="ExternalOutput").ap())
    gps_layer_kernel(nc, *args)
    r = run_bass_kernel_spmd(nc, [arrays], core_ids=[0])
    return r.results[0]["out_x"]
```
